# Optimizing a Trainium2 kernel written in Bass

```python
import numpy as np
import jax
import jax.numpy as jnp

def _softmax(x, axis=-1):
    return jax.nn.softmax(x, axis=axis)

def _gelu(x):
    return jax.nn.gelu(x, approximate=True)

def _silu(x):
    return jax.nn.silu(x)

def _sigmoid(x):
    return jax.nn.sigmoid(x)

def _layernorm(x, axis=-1, eps=1e-05):
    m = jnp.mean(x, axis=axis, keepdims=True)
    v = jnp.var(x, axis=axis, keepdims=True)
    return (x - m) / jnp.sqrt(v + eps)

def _scatter_add(tgt, idx, src, axis=0):
    return tgt.at[idx].add(src)

def _segment_sum(src, seg, n):
    return jax.ops.segment_sum(src, seg, n)
kernel_name = 'mk_adj_ffn_d1_adj_r2_2343b5'

def setup_inputs(seed: int=0):
    np.random.seed(seed)
    _w = jnp.asarray

    def _rec_inputs():
        import jax
        import jax.numpy as jnp
        _gk = jax.random.key(seed)
        x = -0.0002928 + 1 * jax.random.normal(jax.random.fold_in(_gk, 1), (2048, 512), jnp.float32)
        _a = jax.random.bernoulli(jax.random.fold_in(_gk, 2), 0.0078125, (2048, 2048))
        _a = jnp.logical_or(_a, jnp.swapaxes(_a, -1, -2))
        _a = jnp.logical_or(_a, jnp.eye(2048, dtype=bool))
        _af = _a.astype(jnp.float32)
        adj = _af
        return (x, adj)
    x, adj = _rec_inputs()

    def _L0_gnn_setup():
        import jax, jax.numpy as jnp
        import numpy as np
        ALPHA = 0.2
        NEG = -9000000000000000.0
        N, NFEAT, NHID, NHEADS = (2048, 512, 64, 8)
        EMB = NHID * NHEADS
        key = jax.random.key(seed)
        ks = jax.random.split(key, 16)
        x = jax.random.normal(ks[0], (N, NFEAT), dtype=jnp.float32)
        adj = (jax.random.uniform(ks[1], (N, N)) < 0.01).astype(jnp.float32)
        adj = jnp.maximum(adj, jnp.eye(N, dtype=jnp.float32))
        s = 0.05
        W = jax.random.normal(ks[2], (NHEADS, NFEAT, NHID), dtype=jnp.float32) * s
        a1 = jax.random.normal(ks[3], (NHEADS, NHID), dtype=jnp.float32) * s
        a2 = jax.random.normal(ks[4], (NHEADS, NHID), dtype=jnp.float32) * s
        W1 = jax.random.normal(ks[5], (EMB // 2, EMB), dtype=jnp.float32) * s
        b1 = jnp.zeros((EMB // 2,), dtype=jnp.float32)
        W2 = jax.random.normal(ks[6], (NFEAT // 4, EMB // 2), dtype=jnp.float32) * s
        b2 = jnp.zeros((NFEAT // 4,), dtype=jnp.float32)
        W3 = jax.random.normal(ks[7], (NFEAT // 2, NFEAT // 4), dtype=jnp.float32) * s
        b3 = jnp.zeros((NFEAT // 2,), dtype=jnp.float32)
        W4 = jax.random.normal(ks[8], (NFEAT, NFEAT // 2), dtype=jnp.float32) * s
        b4 = jnp.zeros((NFEAT,), dtype=jnp.float32)
        return {'x': x, 'adj': adj, 'W': W, 'a1': a1, 'a2': a2, 'W1': W1, 'b1': b1, 'W2': W2, 'b2': b2, 'W3': W3, 'b3': b3, 'W4': W4, 'b4': b4}
    _L0_gnn_all = _L0_gnn_setup()
    _L0_gnn_in = {k: v for k, v in _L0_gnn_all.items() if k in ('W', 'a1', 'a2', 'W1', 'b1', 'W2', 'b2', 'W3', 'b3', 'W4', 'b4')}
    del _L0_gnn_all

    def _L0_ffn_setup():
        import jax, jax.numpy as jnp
        import numpy as np
        B, S, D, E, K = (4, 1024, 512, 8, 2)
        EPS, W_THRES, TEMP = (0.0001, 0.1, 1.0)
        key = jax.random.key(seed)
        k1, k2, k3, k4, k5 = jax.random.split(key, 5)
        x = jax.random.normal(k1, (B, S, D), dtype=jnp.float32)
        gate_W = jax.random.normal(k2, (D, E), dtype=jnp.float32) * 0.02
        gate_b = jnp.zeros((E,), dtype=jnp.float32)
        expert_W = jax.random.normal(k3, (E, D, D), dtype=jnp.float32) * 0.02
        expert_b = jnp.zeros((E, D), dtype=jnp.float32)
        return {'x': x, 'gate_W': gate_W, 'gate_b': gate_b, 'expert_W': expert_W, 'expert_b': expert_b}
    _L0_ffn_all = _L0_ffn_setup()
    _L0_ffn_in = {k: v for k, v in _L0_ffn_all.items() if k in ('gate_W', 'gate_b', 'expert_W', 'expert_b')}
    del _L0_ffn_all
    return {'x': x, 'adj': adj, 'L0_gnn_W': _L0_gnn_in['W'], 'L0_gnn_a1': _L0_gnn_in['a1'], 'L0_gnn_a2': _L0_gnn_in['a2'], 'L0_gnn_W1': _L0_gnn_in['W1'], 'L0_gnn_b1': _L0_gnn_in['b1'], 'L0_gnn_W2': _L0_gnn_in['W2'], 'L0_gnn_b2': _L0_gnn_in['b2'], 'L0_gnn_W3': _L0_gnn_in['W3'], 'L0_gnn_b3': _L0_gnn_in['b3'], 'L0_gnn_W4': _L0_gnn_in['W4'], 'L0_gnn_b4': _L0_gnn_in['b4'], 'L0_ffn_gate_W': _L0_ffn_in['gate_W'], 'L0_ffn_gate_b': _L0_ffn_in['gate_b'], 'L0_ffn_expert_W': _L0_ffn_in['expert_W'], 'L0_ffn_expert_b': _L0_ffn_in['expert_b']}

def reference(x, adj, L0_gnn_W, L0_gnn_a1, L0_gnn_a2, L0_gnn_W1, L0_gnn_b1, L0_gnn_W2, L0_gnn_b2, L0_gnn_W3, L0_gnn_b3, L0_gnn_W4, L0_gnn_b4, L0_ffn_gate_W, L0_ffn_gate_b, L0_ffn_expert_W, L0_ffn_expert_b):
    import jax
    import jax.numpy as jnp

    def _L0_gnn_ref(x, adj, W, a1, a2, W1, b1, W2, b2, W3, b3, W4, b4):
        import jax, jax.numpy as jnp
        import numpy as np
        ALPHA = 0.2
        NEG = -9000000000000000.0
        N, NFEAT, NHID, NHEADS = (2048, 512, 64, 8)
        EMB = NHID * NHEADS
        Wh = jnp.einsum('nf,hfd->hnd', x, W)
        e_src = jnp.einsum('hnd,hd->hn', Wh, a1)
        e_dst = jnp.einsum('hnd,hd->hn', Wh, a2)
        e = jax.nn.leaky_relu(e_src[:, :, None] + e_dst[:, None, :], ALPHA)
        e = jnp.where(adj[None] > 0, e, NEG)
        att = jax.nn.softmax(e, axis=-1)
        h = jnp.einsum('hnm,hmd->hnd', att, Wh)
        h = jax.nn.elu(h)
        enc = jnp.transpose(h, (1, 0, 2)).reshape(x.shape[0], -1)
        out = jax.nn.relu(enc @ W1.T + b1)
        out = jax.nn.relu(out @ W2.T + b2)
        out = jax.nn.relu(out @ W3.T + b3)
        out = out @ W4.T + b4
        return out

    def _L0_ffn_ref(x, gate_W, gate_b, expert_W, expert_b):
        import jax, jax.numpy as jnp
        import numpy as np
        B, S, D, E, K = (4, 1024, 512, 8, 2)
        EPS, W_THRES, TEMP = (0.0001, 0.1, 1.0)
        scores = jnp.maximum((x @ gate_W + gate_b) / TEMP, EPS)
        p = jax.nn.softmax(scores, axis=-1)
        _, topk_idx = jax.lax.top_k(p, K)
        topk_mask = jax.nn.one_hot(topk_idx, E, dtype=p.dtype).sum(-2) > 0
        w = jnp.maximum(p, W_THRES)
        w_gather = jnp.take_along_axis(w, topk_idx, axis=-1)
        total = jax.lax.stop_gradient(w_gather.sum(-1, keepdims=True))
        w = w / total
        comb = jnp.where(topk_mask, w, jnp.zeros_like(w))
        y = jnp.einsum('bsd,edf->bsef', x, expert_W) + expert_b
        out = jnp.einsum('bsef,bse->bsf', y, comb) / K
        return out
    x = x + _L0_gnn_ref(_layernorm(x, axis=-1), adj, L0_gnn_W, L0_gnn_a1, L0_gnn_a2, L0_gnn_W1, L0_gnn_b1, L0_gnn_W2, L0_gnn_b2, L0_gnn_W3, L0_gnn_b3, L0_gnn_W4, L0_gnn_b4)
    x = x + _L0_ffn_ref(_layernorm(x, axis=-1)[None], L0_ffn_gate_W, L0_ffn_gate_b, L0_ffn_expert_W, L0_ffn_expert_b)[0]
    return x

_drawn_inputs = setup_inputs


def setup_inputs(seed=0):
    import zlib

    import numpy as np

    out = dict(_drawn_inputs(seed))
    spreads = {'L0_gnn_b1': (0.0, 0.363),
     'L0_gnn_b2': (0.0, 0.1),
     'L0_gnn_b3': (0.0, 0.1),
     'L0_gnn_b4': (0.0, 0.1),
     'L0_ffn_gate_b': (0.0, 0.1),
     'L0_ffn_expert_b': (0.0, 0.1)}
    factors = {'L0_gnn_a1': 8.0, 'L0_gnn_a2': 3.61}
    for name, (base, spread) in spreads.items():
        noise = np.random.default_rng([zlib.crc32(name.encode()), seed]).standard_normal(out[name].shape)
        drawn = base * np.exp(spread * noise) if base else spread * noise
        out[name] = jnp.asarray(drawn.astype(out[name].dtype))
    for name, factor in factors.items():
        out[name] = (out[name] * factor).astype(out[name].dtype)
    return out
```

```python
from contextlib import ExitStack

import concourse.bass as bass
from concourse import mybir

ALU = mybir.AluOpType
ACT = mybir.ActivationFunctionType
AX = mybir.AxisListType
F32 = mybir.dt.float32
F32R = mybir.dt.float32r
BF16 = mybir.dt.bfloat16
RMAX = bass.bass_isa.ReduceOp.max

P = 128
N = 2048
F = 512
H = 8
D = 64
DX = D + 1
NT = N // P
KF = F // P
CH = 512
NC = N // CH
TC = CH // P
E = 8
PARTS = 3
JG = 4
NG = NT // JG
F1, F2, F3 = 256, 128, 256
ALPHA = 0.2
LN_EPS = 1e-5
GATE_EPS = 1e-4
W_THRES = 0.1
TOPK = 2
STEEP = float(2 ** 64)


def layer_kernel(nc, x, adj_t, w, a1, a2, w1, b1, w2, b2, w3, b3, w4, b4,
                 gate_w, gate_b, expert_w, expert_b, ident, head_pick, before, out):
    with ExitStack() as whole:
        def sb(stack, name, shape, dt=F32):
            return stack.enter_context(nc.sbuf_tensor(name, shape, dt))

        def ps(stack, name, shape, dt=F32):
            return stack.enter_context(nc.psum_tensor(name, shape, dt))

        def sem(name):
            return whole.enter_context(nc.semaphore(name))

        carried = sem("carried")
        id_sb = sb(whole, "id_sb", [P, P])
        x_tiles = x.rearrange("(t p) f -> p t f", p=P)
        out_tiles = out.rearrange("(t p) f -> p t f", p=P)
        adj_tiles = adj_t.rearrange("(t p) i -> p t i", p=P)

        num = sb(whole, "num", [P, NT, H, DX])
        colsum = sb(whole, "colsum", [P, H, DX])

        attention = ExitStack()
        scale = sb(attention, "scale", [P, NT, H, 2])
        adj_bf = sb(attention, "adj_bf", [P, 2, NT, CH], BF16)
        steep_d = sb(attention, "steep_d", [P, NT, H])
        s_rows3 = sb(attention, "s_rows3", [96, N], BF16)
        pick = sb(attention, "pick", [96, H, P], BF16)
        adj_in = sb(attention, "adj_in", [P, 2, CH])

        rows = sb(attention, "rows", [2 * H, N])
        with ExitStack() as st:
            xs = sb(st, "xs", [P, NT, F])
            xt_hi = sb(st, "xt_hi", [P, 2, KF, CH], F32R)
            xt_lo = sb(st, "xt_lo", [P, 2, KF, CH], F32R)
            xn = sb(st, "xn", [P, TC, F])
            w_raw = sb(st, "w_raw", [P, KF, F])
            w_hi = sb(st, "w_hi", [P, KF, F], F32R)
            w_lo = sb(st, "w_lo", [P, KF, F], F32R)
            a_in = sb(st, "a_in", [P, 2, F])
            wa_prod = sb(st, "wa_prod", [P, KF, F])
            wa = sb(st, "wa", [P, KF, 2 * H])
            wa_hi = sb(st, "wa_hi", [P, KF, 2 * H], F32R)
            wa_lo = sb(st, "wa_lo", [P, KF, 2 * H], F32R)
            stats = sb(st, "stats", [P, TC, 6])
            mv = sb(st, "mv", [P, TC, 2])
            rstd = sb(st, "rstd", [P, TC])
            half = sb(st, "half", [P, TC])
            eps = sb(st, "eps", [P, TC])
            p_x = ps(st, "p_x", [P, KF, CH])
            p_wh = ps(st, "p_wh", [P, 2, F])
            p_rows = ps(st, "p_rows", [2 * H, CH])

            id_in, w_in, a_in_s = sem("id_in"), sem("w_in"), sem("a_in_s")
            x_in = [sem("x_in0"), sem("x_in1")]
            a0_in, a0_read = sem("a0_in"), sem("a0_read")
            whi_done, wlo_done, wa_step, wa_cut = sem("whi_done"), sem("wlo_done"), sem("wa_step"), sem("wa_cut")
            half_done, var_done, mean_done, rstd_done, xn_done = (
                sem("half_done"), sem("var_done"), sem("mean_done"), sem("rstd_done"), sem("xn_done"))
            xt_done, xhi_done, xlo_done = sem("xt_done"), sem("xhi_done"), sem("xlo_done")
            wh_done, wh_out, rows_done, rows_out = sem("wh_done"), sem("wh_out"), sem("rows_done"), sem("rows_out")
            ones_done = sem("ones_done")

            with nc.Block() as block:
                @block.sync
                def _(sp):
                    for g in range(2):
                        sp.dma_start(xs[:, g * TC:(g + 1) * TC, :], x_tiles[:, g * TC:(g + 1) * TC, :]).then_inc(x_in[g], 16)
                    sp.dma_start(id_sb[:], ident).then_inc(id_in, 16)
                    sp.dma_start(w_raw[:], w.rearrange("(k p) c -> p k c", p=P)).then_inc(w_in, 16)
                    sp.dma_start(a_in[:, 0, :], a1.partition_broadcast(P)).then_inc(a_in_s, 16)
                    sp.dma_start(a_in[:, 1, :], a2.partition_broadcast(P)).then_inc(a_in_s, 16)
                    for g in range(2, NC):
                        sp.wait_ge(x_in[g % 2], 16)
                        sp.dma_start(xs[:, g * TC:(g + 1) * TC, :], x_tiles[:, g * TC:(g + 1) * TC, :]).then_inc(x_in[g % 2], 16)
                    sp.dma_start(adj_in[:], adj_tiles[:, 0:2, 0:CH]).then_inc(a0_in, 16)
                    with sp.Fori(1, NT // 2) as j:
                        sp.wait_ge(a0_read, j)
                        sp.dma_start(adj_in[:], adj_tiles[:, bass.ds(j * 2, 2), 0:CH]).then_inc(a0_in, 16)

                @block.gpsimd
                def _(pool):
                    pool.memset(half[:], -0.5).then_inc(half_done, 1)
                    pool.memset(eps[:], LN_EPS).then_inc(half_done, 1)
                    pool.memset(num[:, :, :, D:DX], 1.0).then_inc(ones_done, 1)
                    pool.memset(colsum[:, :, D:DX], float(N)).then_inc(ones_done, 1)
                    pool.wait_ge(half_done, 2)

                    def group(k):
                        pool.wait_ge(mean_done, TC * (k + 1))
                        pool.tensor_tensor(rstd[:], mv[:, :, 1], eps[:], ALU.add).then_inc(var_done, 1)
                        pool.wait_ge(var_done, k + 1)
                        pool.tensor_tensor(rstd[:], rstd[:], half[:], ALU.pow).then_inc(rstd_done, 1)

                    with pool.Fori(0, NC) as k:
                        group(k)
                    for j in range(NT // 2):
                        pool.wait_ge(a0_in, 16 * (j + 1))
                        pool.tensor_scalar(adj_bf[:, 0, j * 2:(j + 1) * 2, :], adj_in[:], 0.0, None, ALU.is_gt).then_inc(a0_read, 1)

                @block.vector
                def _(dve):
                    def group(gg, b):
                        k = gg * 2 + b
                        dve.wait_ge(x_in[b], 16 * (gg + 1))
                        dve.sem_inc(carried, 1)
                        for u in range(TC):
                            dve.bn_stats(stats[:, u, :], xs[:, bass.ds(k * TC + u, 1), :].rearrange("p a f -> p (a f)")).then_inc(wa_step, 1)
                        for u in range(TC):
                            dve.wait_ge(wa_step, k * TC + u + 5)
                            dve.sem_inc(carried, 1)
                            dve.bn_aggr(mv[:, u, :], stats[:, u, :]).then_inc(mean_done, 1)
                        dve.wait_ge(rstd_done, k + 1)
                        for u in range(TC):
                            xv = xs[:, bass.ds(k * TC + u, 1), :].rearrange("p a f -> p (a f)")
                            dve.tensor_scalar(xn[:, u, :], xv, mv[:, u, 0:1], rstd[:, u:u + 1], ALU.subtract, ALU.mult).then_inc(xn_done, 1)
                        for f in range(KF):
                            dve.wait_ge(xhi_done, k * KF + f + 1)
                            dve.tensor_tensor(xt_lo[:, b, f, :], p_x[:, f, :], xt_hi[:, b, f, :].bitcast(F32),
                                              ALU.subtract).then_inc(xlo_done, 1)

                    dve.wait_ge(w_in, 16)
                    dve.wait_ge(a_in_s, 32)
                    for i in range(2):
                        if i:
                            dve.wait_ge(wa_step, 2)
                        dve.tensor_tensor(wa_prod[:], w_raw[:], a_in[:, i:i + 1, :].broadcast_to([P, KF, F]),
                                          ALU.mult).then_inc(wa_step, 1)
                        dve.wait_ge(wa_step, 2 * i + 1)
                        dve.tensor_reduce(wa[:, :, i * H:(i + 1) * H], wa_prod[:].rearrange("p k (h d) -> p k h d", h=H),
                                          AX.X, ALU.add).then_inc(wa_step, 1)
                    dve.wait_ge(whi_done, 1)
                    dve.tensor_tensor(w_lo[:], w_raw[:], w_hi[:].bitcast(F32), ALU.subtract).then_inc(wlo_done, 1)
                    dve.wait_ge(wa_step, 4)
                    dve.tensor_copy(wa_hi[:], wa[:]).then_inc(wa_cut, 1)
                    dve.wait_ge(wa_cut, 1)
                    dve.tensor_tensor(wa_lo[:], wa[:], wa_hi[:].bitcast(F32), ALU.subtract).then_inc(wa_cut, 1)
                    with dve.Fori(0, NC // 2) as gg:
                        for b in range(2):
                            group(gg, b)

                @block.scalar
                def _(act):
                    act.wait_ge(w_in, 16)
                    act.activation(w_hi[:], w_raw[:], ACT.Copy).then_inc(whi_done, 1)

                    def group(gg, b):
                        k = gg * 2 + b
                        for f in range(KF):
                            act.wait_ge(xt_done, k * KF + f + 1)
                            act.activation(xt_hi[:, b, f, :], p_x[:, f, :], ACT.Copy).then_inc(xhi_done, 1)
                        act.wait_ge(rows_done, k + 1)
                        act.activation(rows[:, bass.ds(k * CH, CH)], p_rows[:], ACT.Copy).then_inc(rows_out, 1)
                        for u in range(TC):
                            act.wait_ge(wh_done, k * TC + u + 1)
                            act.activation(num[:, bass.ds(k * TC + u, 1), :, 0:D].rearrange("p a h d -> p (a h) d"),
                                           p_wh[:, u % 2, :].rearrange("p (h d) -> p h d", h=H), ACT.Copy).then_inc(wh_out, 1)

                    with act.Fori(0, NC // 2) as gg:
                        for b in range(2):
                            group(gg, b)

                @block.tensor
                def _(pe):
                    pe.wait_ge(id_in, 16)

                    def turn(k):
                        for u in range(TC):
                            pe.wait_ge(xn_done, k * TC + u + 1)
                            for f in range(KF):
                                mm = pe.transpose(p_x[:, f, u * P:(u + 1) * P],
                                                  xn[:, u, f * P:(f + 1) * P], id_sb[:])
                                if u == TC - 1:
                                    mm.then_inc(xt_done, 1)

                    def products(k, b, first):
                        pe.wait_ge(xlo_done, (k + 1) * KF)
                        if not first:
                            pe.wait_ge(rows_out, k)
                        for n, (l, r) in enumerate([(wa_hi, xt_hi), (wa_hi, xt_lo), (wa_lo, xt_hi)]):
                            for f in range(KF):
                                mm = pe.matmul(p_rows[:], l[:, f, :], r[:, b, f, :], start=(n + f == 0), stop=(n == 2 and f == KF - 1))
                        mm.then_inc(rows_done, 1)
                        for u in range(TC):
                            if not (first and u < 2):
                                pe.wait_ge(wh_out, k * TC + u - 1)
                            for f in range(KF):
                                hi, lo = (t[:, b, f, u * P:(u + 1) * P] for t in (xt_hi, xt_lo))
                                pe.matmul(p_wh[:, u % 2, :], hi, w_hi[:, f, :], start=(f == 0), stop=False)
                                pe.matmul(p_wh[:, u % 2, :], hi, w_lo[:, f, :], start=False, stop=False)
                                mm = pe.matmul(p_wh[:, u % 2, :], lo, w_hi[:, f, :], start=False, stop=(f == KF - 1))
                            mm.then_inc(wh_done, 1)

                    turn(0)
                    pe.wait_ge(wlo_done, 1)
                    pe.wait_ge(wa_cut, 2)
                    products(0, 0, True)
                    pe.wait_ge(xlo_done, KF)
                    turn(1)
                    products(1, 1, False)
                    with pe.Fori(1, NC // 2) as gg:
                        for b in range(2):
                            turn(gg * 2 + b)
                            products(gg * 2 + b, b, False)

        uv = sb(attention, "uv", [P, NT, H, 2, PARTS, DX], BF16)
        with ExitStack() as st:
            sd = sb(st, "sd", [P, NT, 2 * H])
            dmax = sb(st, "dmax", [P, H])
            dtop = sb(st, "dtop", [P, H])
            ex = sb(st, "ex", [P, 2, NT, H])
            q = sb(st, "q", [P, NT, H])
            m = sb(st, "m", [P, NT, H])
            arg = sb(st, "arg", [P, NT, H, 2])
            ones = sb(st, "ones", [P, P])
            part2 = sb(st, "part2", [H, N], BF16)
            pick_in = sb(st, "pick_in", [96, H * P])
            wgt = sb(st, "wgt", [P, 2, 2, H, DX])
            p_sd = ps(st, "p_sd", [P, NT, 2 * H])
            p_cs = ps(st, "p_cs", [P, F])
            sd_done, sd_out, dmax_done, dtop_done = sem("sd_done"), sem("sd_out"), sem("dmax_done"), sem("dtop_done")
            arg_done, m_step, ex_done, scale_done = sem("arg_done"), sem("m_step"), sem("ex_done"), sem("scale_done")
            rest_s, p1_s, p2_s, zero_s, pick_s, pickb_s = (sem("rest_s"), sem("p1_s"), sem("p2_s"), sem("zero_s"),
                                                          sem("pick_s"), sem("pickb_s"))
            ones_s, cs_done, cs_out = sem("ones_s"), sem("cs_done"), sem("cs_out")
            wgt_done, cut1, rest1, cut2, cut3 = sem("wgt_done"), sem("cut1"), sem("rest1"), sem("cut2"), sem("cut3")
            with nc.Block() as block:
                @block.sync
                def _(sp):
                    sp.dma_start(pick_in[:], head_pick).then_inc(pick_s, 16)

                @block.tensor
                def _(pe):
                    for t in range(NT):
                        mm = pe.transpose(p_sd[:, t, :], rows[:, t * P:(t + 1) * P], id_sb[0:2 * H, 0:2 * H])
                    mm.then_inc(sd_done, 1)
                    pe.wait_ge(ones_s, 1)
                    for t in range(NT):
                        mm = pe.matmul(p_cs[:], ones[:], num[:, t, :, 0:D], start=(t == 0), stop=(t == NT - 1))
                    mm.then_inc(cs_done, 1)

                @block.vector
                def _(dve):
                    dve.memset(ones[:], 1.0).then_inc(ones_s, 1)
                    dve.memzero(s_rows3[:].bitcast(mybir.dt.uint32)).then_inc(zero_s, 1)
                    dve.wait_ge(sd_done, 1)
                    dve.tensor_copy(sd[:], p_sd[:]).then_inc(sd_out, 1)
                    dve.wait_ge(sd_out, 1)
                    dve.tensor_reduce(dmax[:], sd[:, :, H:2 * H].rearrange("p t h -> p h t"), AX.X, ALU.max).then_inc(dmax_done, 1)
                    dve.tensor_scalar(steep_d[:], sd[:, :, H:2 * H], STEEP, None, ALU.mult).then_inc(m_step, 1)
                    dve.wait_ge(dtop_done, 1)
                    top = dtop[:].rearrange("p (a h) -> p a h", a=1).broadcast_to([P, NT, H])
                    dve.tensor_tensor(ex[:, 0], sd[:, :, H:2 * H], top, ALU.subtract).then_inc(arg_done, 1)
                    dve.tensor_tensor(q[:], sd[:, :, 0:H], top, ALU.add).then_inc(m_step, 1)
                    dve.wait_ge(m_step, 2)
                    dve.scalar_tensor_tensor(m[:], q[:], ALPHA, q[:], ALU.mult, ALU.max).then_inc(m_step, 1)
                    dve.wait_ge(m_step, 3)
                    dve.tensor_tensor(arg[:, :, :, 0], q[:], m[:], ALU.subtract).then_inc(m_step, 1)
                    dve.scalar_tensor_tensor(arg[:, :, :, 1], q[:], ALPHA, m[:], ALU.mult, ALU.subtract).then_inc(m_step, 1)

                    dve.sem_inc(rest1, 2)
                    dve.sem_inc(cut3, 2)
                    with dve.Fori(0, NT) as t:
                        for s in range(2):
                            dve.wait_ge(cut1, 2 * t + s + 1)
                            dve.wait_ge(cut3, 2 * t + s + 1)
                            first = uv[:, bass.ds(t, 1), :, s, 0, :].rearrange("p a h d -> p (a h) d")
                            dve.tensor_tensor(wgt[:, 1, s], wgt[:, 0, s], first, ALU.subtract).then_inc(rest1, 1)
                        for s in range(2):
                            dve.wait_ge(cut2, 2 * t + s + 1)
                            second, third = (uv[:, bass.ds(t, 1), :, s, i, :].rearrange("p a h d -> p (a h) d") for i in (1, 2))
                            dve.tensor_tensor(third, wgt[:, 1, s], second, ALU.subtract).then_inc(cut3, 1)

                    dve.wait_ge(p1_s, 1)
                    dve.tensor_tensor(rows[0:H, :], rows[0:H, :], s_rows3[0:H, :], ALU.subtract).then_inc(rest_s, 1)
                    dve.wait_ge(rest_s, 1)
                    dve.tensor_copy(part2[:], rows[0:H, :]).then_inc(rest_s, 1)
                    dve.wait_ge(rest_s, 2)
                    dve.tensor_tensor(rows[0:H, :], rows[0:H, :], part2[:], ALU.subtract).then_inc(rest_s, 1)
                    dve.wait_ge(rest_s, 3)
                    dve.tensor_copy(s_rows3[64:64 + H, :], rows[0:H, :]).then_inc(rest_s, 1)
                    dve.wait_ge(cs_done, 1)
                    dve.tensor_copy(colsum[:, :, 0:D], p_cs[:].rearrange("p (h d) -> p h d", h=H)).then_inc(cs_out, 1)

                @block.gpsimd
                def _(pool):
                    pool.wait_ge(dmax_done, 1)
                    pool.partition_all_reduce(dtop[:], dmax[:], P, RMAX).then_inc(dtop_done, 1)
                    pool.wait_ge(ex_done, 2)
                    with pool.Fori(0, NT) as t:
                        for s in range(2):
                            pool.wait_ge(rest1, 2 * t + s + 1)
                            pool.tensor_tensor(wgt[:, 0, s], num[:, bass.ds(t, 1), :, :].rearrange("p a h d -> p (a h) d"),
                                               ex[:, s, bass.ds(t, 1), :].rearrange("p a h -> p (a h)").unsqueeze(2).broadcast_to([P, H, DX]),
                                               ALU.mult).then_inc(wgt_done, 1)

                @block.scalar
                def _(act):
                    act.wait_ge(zero_s, 1)
                    act.activation(s_rows3[0:H, :], rows[0:H, :], ACT.Copy).then_inc(p1_s, 1)
                    act.wait_ge(arg_done, 1)
                    act.activation(ex[:, 1], ex[:, 0], ACT.Exp, scale=ALPHA).then_inc(ex_done, 1)
                    act.wait_ge(ex_done, 1)
                    act.activation(ex[:, 0], ex[:, 0], ACT.Exp).then_inc(ex_done, 1)
                    act.wait_ge(m_step, 5)
                    act.activation(scale[:], arg[:], ACT.Exp).then_inc(scale_done, 1)
                    with act.Fori(0, NT) as t:
                        for s in range(2):
                            act.wait_ge(wgt_done, 2 * t + s + 1)
                            act.activation(uv[:, bass.ds(t, 1), :, s, 0, :].rearrange("p a h d -> p (a h) d"),
                                           wgt[:, 0, s], ACT.Copy).then_inc(cut1, 1)
                        for s in range(2):
                            act.wait_ge(rest1, 2 * t + s + 3)
                            act.activation(uv[:, bass.ds(t, 1), :, s, 1, :].rearrange("p a h d -> p (a h) d"),
                                           wgt[:, 1, s], ACT.Copy).then_inc(cut2, 1)
                    act.wait_ge(pick_s, 16)
                    act.activation(pick[:], pick_in[:].rearrange("p (h c) -> p h c", h=H), ACT.Copy).then_inc(pickb_s, 1)
                    act.wait_ge(rest_s, 2)
                    act.activation(s_rows3[32:32 + H, :], part2[:], ACT.Copy).then_inc(p2_s, 1)


        RB = 2
        HT = NG * TC
        with ExitStack() as st:
            m1 = sb(st, "m1", [P, RB, JG, CH], BF16)
            m0 = sb(st, "m0", [P, RB, JG, CH], BF16)
            sums = sb(st, "sums", [P, 2, TC, 2, DX])
            fill = sb(st, "fill", [P, CH], BF16)
            p_acc = ps(st, "p_acc", [P, TC, CH])
            p_s = ps(st, "p_s", [P, 2, CH])
            adj_in_s, conv_done = sem("adj_in_s"), sem("conv_done")
            s_ready, relu_done, m1_ready, m1_used, m0_ready = (
                sem("s_ready"), sem("relu_done"), sem("m1_ready"), sem("m1_used"), sem("m0_ready"))
            tiles_done, acc_read, sums_used, scaled, fill_s = (
                sem("tiles_done"), sem("acc_read"), sem("sums_used"), sem("scaled"), sem("fill_s"))
            DXX = 2 * PARTS * DX

            def heads(eng, body):
                with eng.Fori(0, NC // 2) as cc:
                    for cb in range(2):
                        with eng.Fori(0, H // 2) as hh:
                            for hb in range(2):
                                body((cc * 2 + cb) * H + hh * 2 + hb, cc * 2 + cb, hh * 2 + hb, hb, cb)

            with nc.Block() as block:
                @block.sync
                def _(sp):
                    for c in range(1, NC):
                        with sp.Fori(0, NT // 2) as j:
                            sp.wait_ge(conv_done, (c - 1) * (NT // 2) + 1 + j)
                            sp.dma_start(adj_in[:], adj_tiles[:, bass.ds(j * 2, 2), c * CH:(c + 1) * CH]).then_inc(adj_in_s, 16)

                @block.gpsimd
                def _(pool):
                    pool.sem_inc(conv_done, 1)
                    pool.sem_inc(sums_used, 3)

                    def scale_head(n, c, h, hb):
                        pool.wait_ge(acc_read, TC * n + 2 * TC)
                        pool.tensor_tensor(sums[:, hb], sums[:, hb],
                                           scale[:, c * TC:(c + 1) * TC, h, :].unsqueeze(3).broadcast_to([P, TC, 2, DX]),
                                           ALU.mult).then_inc(scaled, 1)
                        pool.wait_ge(scaled, n + 1)
                        pool.tensor_tensor(num[:, c * TC:(c + 1) * TC, h, :],
                                           sums[:, hb, :, 0, :], sums[:, hb, :, 1, :], ALU.add).then_inc(sums_used, 1)

                    for c in range(NC):
                        if c >= 1 and c < NC - 1:
                            pool.wait_ge(m0_ready, c * H * NG + RB)
                        for h in range(H):
                            if c < NC - 1:
                                pool.wait_ge(adj_in_s, (c * H + 1 + h) * 16)
                                pool.tensor_scalar(adj_bf[:, (c + 1) % 2, h * 2:(h + 1) * 2, :], adj_in[:], 0.0, None,
                                                   ALU.is_gt).then_inc(conv_done, 1)
                            scale_head(h + c * H, c, h, h % 2)

                @block.scalar
                def _(act):
                    act.sem_inc(relu_done, 2 * NG * JG)

                    def body(n, c, h, hb, cb):
                        act.wait_ge(s_ready, n + 1)
                        for g in range(NG):
                            act.wait_ge(m1_used, n * NG + g + 1)
                            act.wait_ge(m0_ready, n * NG + g + 1)
                            for j in range(JG):
                                t = g * JG + j
                                act.activation(m1[:, g % RB, j, :], p_s[:, hb, :], ACT.Relu, scale=STEEP,
                                               bias=steep_d[:, t, bass.ds(h, 1)]).then_inc(relu_done, 1)

                    heads(act, body)

                @block.vector
                def _(dve):
                    dve.sem_inc(m0_ready, RB)
                    dve.memset(fill[:], 0.0).then_inc(fill_s, 1)

                    def evacuate(n, hb):
                        dve.wait_ge(sums_used, n + 1)
                        for i in range(TC):
                            dve.wait_ge(tiles_done, n * HT + TC + i + 1)
                            dve.tensor_reduce(sums[:, 1 - hb, i], p_acc[:, i, 0:DXX].rearrange("p (m k d) -> p m d k", m=2, k=PARTS),
                                              AX.X, ALU.add).then_inc(acc_read, 1)

                    def body(n, c, h, hb, cb):
                        dve.wait_ge(conv_done, c * (NT // 2) + 1)
                        for g in range(NG):
                            edges = adj_bf[:, cb, g * JG:(g + 1) * JG, :]
                            dve.wait_ge(relu_done, (n * NG + g) * JG + (2 * NG + 1) * JG)
                            dve.tensor_tensor(m1[:, g % RB], m1[:, g % RB], edges, ALU.min).then_inc(m1_ready, 1)
                            dve.wait_ge(tiles_done, (n * NG + g) * TC + TC)
                            dve.wait_ge(m1_ready, n * NG + g + 1)
                            dve.tensor_tensor(m0[:, g % RB], edges, m1[:, g % RB], ALU.subtract).then_inc(m0_ready, 1)
                            if g == 0:
                                evacuate(n, hb)

                    heads(dve, body)
                    evacuate(NC * H, 0)

                @block.tensor
                def _(pe):
                    pe.sem_inc(m1_used, RB)
                    pe.sem_inc(tiles_done, TC)
                    pe.wait_ge(fill_s, 1)
                    for i in range(TC):
                        pe.matmul(p_acc[:, i, :], fill[:, 0:P], fill[:], start=True, stop=True).then_inc(tiles_done, 1)

                    def body(n, c, h, hb, cb):
                        pe.wait_ge(relu_done, n * NG * JG + NG * JG)
                        pe.matmul(p_s[:, hb, :], pick[:, bass.ds(h, 1), :].rearrange("p a c -> p (a c)"),
                                  s_rows3[:, bass.ds(c * CH, CH)], start=True, stop=True).then_inc(s_ready, 1)
                        for g in range(NG):
                            pe.wait_ge(m1_ready, n * NG + g + 1)
                            for j in range(JG):
                                for i in range(TC):
                                    if g == 0 and j == 0:
                                        pe.wait_ge(acc_read, n * TC + i + 1)
                                    mm = pe.matmul(p_acc[:, i, 0:DXX // 2], m1[:, g % RB, j, i * P:(i + 1) * P],
                                                   uv[:, g * JG + j, bass.ds(h, 1), 0].rearrange("p a k d -> p (a k d)"),
                                                   start=(g == 0 and j == 0), stop=False, skip_group_check=True)
                            mm.then_inc(m1_used, 1)
                            pe.wait_ge(m0_ready, n * NG + g + 1 + RB)
                            for j in range(JG):
                                for i in range(TC):
                                    mm = pe.matmul(p_acc[:, i, DXX // 2:DXX], m0[:, g % RB, j, i * P:(i + 1) * P],
                                                   uv[:, g * JG + j, bass.ds(h, 1), 1].rearrange("p a k d -> p (a k d)"),
                                                   start=False, stop=(g == NG - 1 and j == JG - 1), skip_group_check=True)
                                    if j == JG - 1:
                                        mm.then_inc(tiles_done, 1)

                    heads(pe, body)
        attention.close()

        late = ExitStack()
        x2 = sb(late, "x2", [P, NT, F])
        x2t_hi = sb(late, "x2t_hi", [P, KF, N], F32R)
        x2t_lo = sb(late, "x2t_lo", [P, KF, N], F32R)
        g_rows = sb(late, "g_rows", [E, N])
        with ExitStack() as st:
            layers = [("w1", w1, F, F1), ("w2", w2, F1, F2), ("w3", w3, F2, F3), ("w4", w4, F3, F), ("gate", gate_w, F, E)]
            cut = {}
            for name, src, k, m_ in layers:
                cut[name] = (sb(st, name + "_hi", [P, k // P, m_], F32R), sb(st, name + "_lo", [P, k // P, m_], F32R))
            b1_sb, b2_sb, b3_sb = sb(st, "b1_sb", [P, F1 // P]), sb(st, "b2_sb", [P, F2 // P]), sb(st, "b3_sb", [P, F3 // P])
            b4_sb = sb(st, "b4_sb", [P, F])
            h_sb = sb(st, "h_sb", [P, TC, F])
            e_sb = sb(st, "e_sb", [P, TC, F])
            et_hi = sb(st, "et_hi", [P, KF, CH], F32R)
            et_lo = sb(st, "et_lo", [P, KF, CH], F32R)
            y_f = sb(st, "y_f", [P, 2, CH])
            y_hi = sb(st, "y_hi", [P, 2, CH], F32R)
            y_lo = sb(st, "y_lo", [P, 2, CH], F32R)
            empty = sb(st, "empty", [P, NT, H])
            add = sb(st, "add", [P, TC, DX])
            rden = sb(st, "rden", [P, TC, H])
            stats = sb(st, "stats2", [P, TC, 6])
            mv = sb(st, "mv2", [P, TC, 2])
            rstd = sb(st, "rstd2", [P, TC])
            half = sb(st, "half2", [P, TC])
            eps = sb(st, "eps2", [P, TC])
            p_t = ps(st, "p_t", [P, KF, CH])
            p_m = ps(st, "p_m", [P, 4, CH])
            empty_s = sem("empty_s")
            raw_in = [sem(f"raw_in{i}") for i in range(5)]
            b_in, raw_hi, raw_lo = sem("b_in"), sem("raw_hi"), sem("raw_lo")
            xb_in, half_s, e_step, fixed, h_step, exp_s = (
                sem("xb_in"), sem("half_s"), sem("e_step"), sem("fixed"), sem("h_step"), sem("exp_s"))
            turned, e_hi, e_lo = sem("turned"), sem("e_hi"), sem("e_lo")
            mm_done, y_act, y_cut = sem("mm_done"), sem("y_act"), sem("y_cut")
            xb_s, x2_s, stat_s, mean_s, var_s, rstd_s = (
                sem("xb_s"), sem("x2_s"), sem("stat_s"), sem("mean_s"), sem("var_s"), sem("rstd_s"))
            xn2_s, turned2, n_hi, n_lo, g_done, g_out = (
                sem("xn2_s"), sem("turned2"), sem("n_hi"), sem("n_lo"), sem("g_done"), sem("g_out"))
            off = 0
            raw = {}
            flat = e_sb[:].rearrange("p t f -> p (t f)")
            flat2 = h_sb[:].rearrange("p t f -> p (t f)")
            for name, src, k, m_ in layers:
                size = k // P * m_
                home, at = (flat, off) if off + size <= TC * F else (flat2, 0)
                raw[name] = home[:, at:at + size].rearrange("p (k m) -> p k m", m=m_)
                off = off + size if home is flat else off
                if home is flat2:
                    flat2 = flat2[:, size:]
            with nc.Block() as block:
                @block.sync
                def _(sp):
                    for i, (name, src, k, m_) in enumerate(layers):
                        sp.dma_start(raw[name], src.rearrange("(k p) m -> p k m", p=P)).then_inc(raw_in[i], 16)
                    for dst, src in ((b1_sb, b1), (b2_sb, b2), (b3_sb, b3)):
                        sp.dma_start(dst[:], src).then_inc(b_in, 16)
                    sp.dma_start(b4_sb[:], b4.partition_broadcast(P)).then_inc(b_in, 16)
                    with sp.Fori(0, NC) as c:
                        sp.wait_ge(h_step, c * 5 + 5)
                        sp.dma_start(e_sb[:], x_tiles[:, bass.ds(c * TC, TC), :]).then_inc(xb_in, 16)

                @block.gpsimd
                def _(pool):
                    pool.memset(half[:], -0.5).then_inc(half_s, 1)
                    pool.memset(eps[:], LN_EPS).then_inc(half_s, 1)
                    pool.wait_ge(b_in, 64)
                    pool.wait_ge(half_s, 2)
                    pool.wait_ge(empty_s, 1)
                    with pool.Fori(0, NC) as c:
                        for h in range(H):
                            part = num[:, bass.ds(c * TC, TC), h, :]
                            pool.tensor_tensor(add[:], colsum[:, h:h + 1, :].broadcast_to([P, TC, DX]),
                                               empty[:, bass.ds(c * TC, TC), h:h + 1].broadcast_to([P, TC, DX]), ALU.mult).then_inc(e_step, 1)
                            pool.wait_ge(e_step, c * 2 * H + 2 * h + 1)
                            pool.tensor_tensor(part, part, add[:], ALU.add).then_inc(e_step, 1)
                            pool.wait_ge(e_step, c * 2 * H + 2 * h + 2)
                        pool.wait_ge(xb_in, 16 * (c + 1))
                        pool.tensor_tensor(e_sb[:], e_sb[:], b4_sb[:].unsqueeze(1).broadcast_to([P, TC, F]), ALU.add).then_inc(xb_s, 1)
                        pool.wait_ge(mean_s, TC * (c + 1))
                        pool.tensor_tensor(rstd[:], mv[:, :, 1], eps[:], ALU.add).then_inc(var_s, 1)
                        pool.wait_ge(var_s, c + 1)
                        pool.tensor_tensor(rstd[:], rstd[:], half[:], ALU.pow).then_inc(rstd_s, 1)

                @block.vector
                def _(dve):
                    for i, (name, src, k, m_) in enumerate(layers):
                        dve.wait_ge(raw_hi, i + 1)
                        dve.tensor_tensor(cut[name][1][:], raw[name], cut[name][0][:].bitcast(F32), ALU.subtract).then_inc(raw_lo, 1)
                    dve.tensor_scalar(empty[:], num[:, :, :, D], 0.0, None, ALU.is_equal).then_inc(empty_s, 1)
                    dve.wait_ge(raw_lo, len(layers))
                    with dve.Fori(0, NC) as c:
                        dve.wait_ge(e_step, (c + 1) * 2 * H)
                        dve.reciprocal(rden[:], num[:, bass.ds(c * TC, TC), :, D]).then_inc(h_step, 1)
                        dve.wait_ge(h_step, c * 5 + 1)
                        heads_out = h_sb[:].rearrange("p t (h d) -> p t h d", h=H)
                        dve.tensor_tensor(heads_out, num[:, bass.ds(c * TC, TC), :, 0:D],
                                          rden[:].unsqueeze(3).broadcast_to([P, TC, H, D]), ALU.mult).then_inc(h_step, 1)
                        dve.wait_ge(h_step, c * 5 + 2)
                        dve.tensor_scalar(e_sb[:], h_sb[:], 0.0, None, ALU.min).then_inc(h_step, 1)
                        dve.wait_ge(exp_s, c + 1)
                        dve.scalar_tensor_tensor(h_sb[:], h_sb[:], 0.0, e_sb[:], ALU.max, ALU.add).then_inc(h_step, 1)
                        dve.wait_ge(h_step, c * 5 + 4)
                        dve.tensor_scalar(h_sb[:], h_sb[:], -1.0, None, ALU.add).then_inc(h_step, 1)
                        for f in range(KF):
                            dve.wait_ge(e_hi, c * KF + f + 1)
                            dve.tensor_tensor(et_lo[:, f, :], p_t[:, f, :], et_hi[:, f, :].bitcast(F32), ALU.subtract).then_inc(e_lo, 1)
                        for n, slot in enumerate((0, 1, 0, 0, 1)):
                            dve.wait_ge(y_act, c * 10 + 2 * n + 2)
                            dve.tensor_tensor(y_lo[:, slot, :], y_f[:, slot, :], y_hi[:, slot, :].bitcast(F32), ALU.subtract).then_inc(y_cut, 1)
                        dve.wait_ge(xb_s, c + 1)
                        for i in range(TC):
                            dve.wait_ge(mm_done, c * 9 + 6 + i)
                            dve.tensor_tensor(x2[:, bass.ds(c * TC + i, 1), :].rearrange("p a f -> p (a f)"),
                                              p_m[:, (1 + i) % 4, :], e_sb[:, i, :], ALU.add).then_inc(x2_s, 1)
                        for i in range(TC):
                            dve.wait_ge(x2_s, c * TC + i + 1)
                            dve.sem_inc(carried, 1)
                            dve.bn_stats(stats[:, i, :], x2[:, bass.ds(c * TC + i, 1), :].rearrange("p a f -> p (a f)")).then_inc(stat_s, 1)
                        for i in range(TC):
                            dve.wait_ge(stat_s, c * TC + i + 1)
                            dve.sem_inc(carried, 1)
                            dve.bn_aggr(mv[:, i, :], stats[:, i, :]).then_inc(mean_s, 1)
                        dve.wait_ge(rstd_s, c + 1)
                        for i in range(TC):
                            dve.tensor_scalar(h_sb[:, i, :], x2[:, bass.ds(c * TC + i, 1), :].rearrange("p a f -> p (a f)"),
                                              mv[:, i, 0:1], rstd[:, i:i + 1], ALU.subtract, ALU.mult).then_inc(xn2_s, 1)
                        for f in range(KF):
                            dve.wait_ge(n_hi, c * KF + f + 1)
                            here = (slice(None), f, bass.ds(c * CH, CH))
                            dve.tensor_tensor(x2t_lo[here], p_t[:, f, :], x2t_hi[here].bitcast(F32), ALU.subtract).then_inc(n_lo, 1)

                @block.scalar
                def _(act):
                    for i, (name, src, k, m_) in enumerate(layers):
                        act.wait_ge(raw_in[i], 16)
                        act.activation(cut[name][0][:], raw[name], ACT.Copy).then_inc(raw_hi, 1)
                    act.wait_ge(b_in, 64)
                    with act.Fori(0, NC) as c:
                        act.wait_ge(h_step, c * 5 + 3)
                        act.activation(e_sb[:], e_sb[:], ACT.Exp).then_inc(exp_s, 1)
                        for f in range(KF):
                            act.wait_ge(turned, c * KF + f + 1)
                            act.activation(et_hi[:, f, :], p_t[:, f, :], ACT.Copy).then_inc(e_hi, 1)
                        for n, (bank, bias, slot) in enumerate([(0, b1_sb[:, 0:1], 0), (1, b1_sb[:, 1:2], 1), (2, b2_sb[:, 0:1], 0),
                                                                (3, b3_sb[:, 0:1], 0), (0, b3_sb[:, 1:2], 1)]):
                            act.wait_ge(mm_done, c * 9 + (5 if n == 3 else n + 1))
                            act.activation(y_f[:, slot, :], p_m[:, bank, :], ACT.Relu, bias=bias).then_inc(y_act, 1)
                            act.activation(y_hi[:, slot, :], p_m[:, bank, :], ACT.Relu, bias=bias).then_inc(y_act, 1)
                        for f in range(KF):
                            act.wait_ge(turned2, c * KF + f + 1)
                            act.activation(x2t_hi[:, f, bass.ds(c * CH, CH)], p_t[:, f, :], ACT.Copy).then_inc(n_hi, 1)
                        act.wait_ge(g_done, c + 1)
                        act.activation(g_rows[:, bass.ds(c * CH, CH)], p_m[0:E, 1, :], ACT.Copy).then_inc(g_out, 1)

                @block.tensor
                def _(pe):
                    pe.wait_ge(raw_lo, len(layers))
                    pe.sem_inc(g_out, 1)

                    def product(dst, name, o, k, hi, lo, m_=P):
                        w_h, w_l = cut[name]
                        for n, (l, r) in enumerate([(w_h, hi), (w_l, hi), (w_h, lo)]):
                            for f in range(k):
                                mm = pe.matmul(dst, l[:, f, o * P:o * P + m_], r(f), start=(n + f == 0), stop=(n == 2 and f == k - 1))
                        return mm

                    with pe.Fori(0, NC) as c:
                        def turn(done):
                            for f in range(KF):
                                for i in range(TC):
                                    mm = pe.transpose(p_t[:, f, i * P:(i + 1) * P], h_sb[:, i, f * P:(f + 1) * P], id_sb[:])
                                mm.then_inc(done, 1)

                        pe.wait_ge(h_step, c * 5 + 5)
                        turn(turned)
                        pe.wait_ge(e_lo, (c + 1) * KF)
                        pe.wait_ge(g_out, c + 1)
                        for o in range(F1 // P):
                            product(p_m[:, o, :], "w1", o, KF, lambda f: et_hi[:, f, :], lambda f: et_lo[:, f, :]).then_inc(mm_done, 1)
                        pe.wait_ge(y_cut, c * 5 + 2)
                        product(p_m[:, 2, :], "w2", 0, 2, lambda f: y_hi[:, f, :], lambda f: y_lo[:, f, :]).then_inc(mm_done, 1)
                        pe.wait_ge(y_cut, c * 5 + 3)
                        for o in range(F3 // P):
                            product(p_m[:, (3 + o) % 4, :], "w3", o, 1, lambda f: y_hi[:, f, :], lambda f: y_lo[:, f, :]).then_inc(mm_done, 1)
                        pe.wait_ge(y_cut, c * 5 + 5)
                        w_h, w_l = cut["w4"]
                        for i in range(TC):
                            dst = p_m[:, (1 + i) % 4, :]
                            for n, (l, r) in enumerate([(y_hi, w_h), (y_hi, w_l), (y_lo, w_h)]):
                                for f in range(2):
                                    mm = pe.matmul(dst, l[:, f, i * P:(i + 1) * P], r[:, f, :], start=(n + f == 0), stop=(n == 2 and f == 1))
                            mm.then_inc(mm_done, 1)
                        pe.wait_ge(xn2_s, (c + 1) * TC)
                        turn(turned2)
                        pe.wait_ge(n_lo, (c + 1) * KF)
                        at = bass.ds(c * CH, CH)
                        product(p_m[0:E, 1, :], "gate", 0, KF, lambda f: x2t_hi[:, f, at], lambda f: x2t_lo[:, f, at], E).then_inc(g_done, 1)

        with ExitStack() as st:
            raw_w = sb(st, "raw_w", [P, 2, KF, F])
            ew_hi = sb(st, "ew_hi", [P, 2, KF, F], F32R)
            ew_lo = sb(st, "ew_lo", [P, 2, KF, F], F32R)
            gb_sb = sb(st, "gb_sb", [P, E])
            tri = sb(st, "tri", [P, E * E])
            eb_sb = sb(st, "eb_sb", [E, F])
            sc = sb(st, "sc", [P, NT, E])
            gt = sb(st, "gt", [P, NT, E, E])
            eq = sb(st, "eq", [P, NT, E, E])
            rank = sb(st, "rank", [P, NT, E])
            col = sb(st, "col", [P, 4, NT])
            pr = sb(st, "pr", [P, NT, E])
            comb_t = g_rows
            p_y = ps(st, "p_y", [P, 4, F])
            p_g = ps(st, "p_g", [P, NT * E])
            p_c = ps(st, "p_c", [E, 3, CH])
            ew_in = [sem("ew_in0"), sem("ew_in1")]
            small_in, ewhi_s, ewlo_s, gt_s, sc_step, ex2_s = (
                sem("small_in"), sem("ewhi_s"), sem("ewlo_s"), sem("gt_s"), sem("sc_step"), sem("ex2_s"))
            ct_done, ct_out, y_done, y_read, out_s = sem("ct_done"), sem("ct_out"), sem("y_done"), sem("y_read"), sem("out_s")
            RING = 4
            with nc.Block() as block:
                @block.sync
                def _(sp):
                    for dst, src in ((gb_sb[:], gate_b.partition_broadcast(P)), (tri[:], before.partition_broadcast(P)), (eb_sb[:], expert_b)):
                        sp.dma_start(dst, src).then_inc(small_in, 16)
                    ew = expert_w.rearrange("e (k p) f -> e p k f", p=P)
                    with sp.Fori(0, E // 2) as ee:
                        for b in range(2):
                            sp.wait_ge(ewlo_s, ee * 2 + b + 1)
                            sp.dma_start(raw_w[:, b], ew[bass.ds(ee * 2 + b, 1)].rearrange("e p k f -> p (e k) f")).then_inc(ew_in[b], 16)
                    for t in range(NT):
                        sp.wait_ge(y_read, RING + (E) * NT + t + 1)
                        sp.dma_start(out_tiles[:, t, :], x2[:, t, :]).then_inc(out_s, 16)
                    sp.wait_ge(out_s, 16 * NT)

                @block.gpsimd
                def _(pool):
                    pool.sem_inc(ewlo_s, 2)
                    with pool.Fori(0, E // 2) as ee:
                        for b in range(2):
                            pool.wait_ge(ewhi_s, ee * 2 + b + 1)
                            pool.tensor_tensor(ew_lo[:, b], raw_w[:, b], ew_hi[:, b].bitcast(F32), ALU.subtract).then_inc(ewlo_s, 1)

                @block.scalar
                def _(act):
                    def cut_hi(ee, b):
                        act.wait_ge(ew_in[b], 16 * (ee + 1))
                        act.wait_ge(y_done, ee * 2 * NT + b * NT + 2 * NT)
                        act.activation(ew_hi[:, b], raw_w[:, b], ACT.Copy).then_inc(ewhi_s, 1)

                    act.sem_inc(y_done, 3 * NT)
                    for b in range(2):
                        cut_hi(0, b)
                    act.wait_ge(sc_step, 7)
                    act.activation(pr[:], pr[:], ACT.Exp).then_inc(ex2_s, 1)
                    with act.Fori(1, E // 2) as ee:
                        for b in range(2):
                            cut_hi(ee, b)

                @block.vector
                def _(dve):
                    steps = [0]

                    def step(ins):
                        steps[0] += 1
                        ins.then_inc(sc_step, 1)
                        dve.wait_ge(sc_step, steps[0])

                    dve.wait_ge(small_in, 48)
                    dve.wait_ge(gt_s, 1)
                    step(dve.tensor_tensor(sc[:], p_g[:].rearrange("p (t e) -> p t e", e=E), gb_sb[:].unsqueeze(1).broadcast_to([P, NT, E]), ALU.add))
                    step(dve.tensor_scalar(sc[:], sc[:], GATE_EPS, None, ALU.max))
                    other = sc[:].unsqueeze(2).broadcast_to([P, NT, E, E])
                    own = sc[:].unsqueeze(3).broadcast_to([P, NT, E, E])
                    step(dve.tensor_tensor(gt[:], other, own, ALU.is_gt))
                    step(dve.tensor_tensor(eq[:], other, own, ALU.is_equal))
                    ones_before = tri[:].rearrange("p (e f) -> p e f", e=E).unsqueeze(1).broadcast_to([P, NT, E, E])
                    step(dve.tensor_tensor(eq[:], eq[:], ones_before, ALU.mult))
                    step(dve.tensor_reduce(col[:, 0, :], sc[:], AX.X, ALU.max))
                    step(dve.tensor_tensor(pr[:], sc[:], col[:, 0, :].unsqueeze(2).broadcast_to([P, NT, E]), ALU.subtract))
                    step(dve.tensor_tensor(gt[:], gt[:], eq[:], ALU.add))
                    step(dve.tensor_reduce(rank[:], gt[:], AX.X, ALU.add))
                    step(dve.tensor_scalar(rank[:], rank[:], float(TOPK), None, ALU.is_lt))
                    dve.wait_ge(ex2_s, 1)
                    step(dve.tensor_reduce(col[:, 1, :], pr[:], AX.X, ALU.add))
                    step(dve.reciprocal(col[:, 1, :], col[:, 1, :]))
                    step(dve.tensor_tensor(pr[:], pr[:], col[:, 1, :].unsqueeze(2).broadcast_to([P, NT, E]), ALU.mult))
                    step(dve.scalar_tensor_tensor(pr[:], pr[:], W_THRES, rank[:], ALU.max, ALU.mult))
                    step(dve.tensor_reduce(col[:, 2, :], pr[:], AX.X, ALU.add))
                    step(dve.tensor_scalar(col[:, 2, :], col[:, 2, :], float(TOPK), None, ALU.mult))
                    step(dve.reciprocal(col[:, 3, :], col[:, 2, :]))
                    step(dve.tensor_tensor(pr[:], pr[:], col[:, 3, :].unsqueeze(2).broadcast_to([P, NT, E]), ALU.mult))

                    def expert(e, first):
                        for t in range(NT):
                            dve.wait_ge(y_done, e * NT + t + 1 + 3 * NT)
                            if not first:
                                dve.wait_ge(y_read, (e - 1) * NT + t + 1 + RING)
                            dve.scalar_tensor_tensor(x2[:, t, :], p_y[:, t % RING, :], pr[:, t, bass.ds(e, 1)], x2[:, t, :],
                                                     ALU.mult, ALU.add).then_inc(y_read, 1)

                    dve.sem_inc(y_read, RING)
                    expert(0, True)
                    for t4 in range(NC):
                        dve.wait_ge(ct_done, t4 + 1)
                        dve.tensor_copy(comb_t[:, t4 * CH:(t4 + 1) * CH], p_c[:, t4 % 3, :]).then_inc(ct_out, 1)
                    with dve.Fori(1, E) as e:
                        expert(e, False)
                    for t in range(NT):
                        dve.wait_ge(y_done, E * NT + t + 1 + 3 * NT)
                        dve.wait_ge(y_read, (E - 1) * NT + t + 1 + RING)
                        dve.tensor_tensor(x2[:, t, :], p_y[:, t % RING, :], x2[:, t, :], ALU.add).then_inc(y_read, 1)

                @block.tensor
                def _(pe):
                    for t in range(NT):
                        mm = pe.transpose(p_g[:, t * E:(t + 1) * E], g_rows[:, t * P:(t + 1) * P], id_sb[0:E, 0:E])
                    mm.then_inc(gt_s, 1)

                    def expert(e, b):
                        pe.wait_ge(ewlo_s, e + 3)
                        for t in range(NT):
                            pe.wait_ge(y_read, e * NT + t + 1)
                            for f in range(KF):
                                hi, lo = x2t_hi[:, f, t * P:(t + 1) * P], x2t_lo[:, f, t * P:(t + 1) * P]
                                pe.matmul(p_y[:, t % RING, :], hi, ew_hi[:, b, f, :], start=(f == 0), stop=False)
                                pe.matmul(p_y[:, t % RING, :], hi, ew_lo[:, b, f, :], start=False, stop=False)
                                mm = pe.matmul(p_y[:, t % RING, :], lo, ew_hi[:, b, f, :], start=False, stop=(f == KF - 1))
                            mm.then_inc(y_done, 1)

                    expert(0, 0)
                    pe.wait_ge(sc_step, 18)
                    for t in range(NT):
                        if t == 3 * TC:
                            pe.wait_ge(ct_out, 1)
                        mm = pe.transpose(p_c[:, t // TC % 3, t % TC * P:(t % TC + 1) * P], pr[:, t, :], id_sb[:])
                        if t % TC == TC - 1:
                            mm.then_inc(ct_done, 1)
                    expert(1, 1)
                    with pe.Fori(1, E // 2) as ee:
                        for b in range(2):
                            expert(ee * 2 + b, b)
                    pe.wait_ge(ct_out, NC)
                    for t in range(NT):
                        pe.wait_ge(y_read, E * NT + t + 1)
                        pe.matmul(p_y[:, t % RING, :], comb_t[:, t * P:(t + 1) * P], eb_sb[:], start=True, stop=True).then_inc(y_done, 1)
        late.close()
    return nc


def kernel(x, adj, L0_gnn_W, L0_gnn_a1, L0_gnn_a2, L0_gnn_W1, L0_gnn_b1, L0_gnn_W2, L0_gnn_b2, L0_gnn_W3, L0_gnn_b3,
           L0_gnn_W4, L0_gnn_b4, L0_ffn_gate_W, L0_ffn_gate_b, L0_ffn_expert_W, L0_ffn_expert_b):
    import numpy as np
    from concourse import bacc
    from concourse.bass_utils import run_bass_kernel_spmd

    head_pick = np.zeros((96, H, P), np.float32)
    for k in range(3):
        for h in range(H):
            head_pick[32 * k + h, h] = 1.0
    arrays = {
        "x": np.asarray(x),
        "adj_t": np.asarray(adj).T,
        "w": np.asarray(L0_gnn_W).transpose(1, 0, 2).reshape(F, H * D),
        "a1": np.asarray(L0_gnn_a1).reshape(-1), "a2": np.asarray(L0_gnn_a2).reshape(-1),
        "w1": np.asarray(L0_gnn_W1).T, "b1": np.asarray(L0_gnn_b1).reshape(-1, P).T,
        "w2": np.asarray(L0_gnn_W2).T, "b2": np.asarray(L0_gnn_b2).reshape(-1, P).T,
        "w3": np.asarray(L0_gnn_W3).T, "b3": np.asarray(L0_gnn_b3).reshape(-1, P).T,
        "w4": np.asarray(L0_gnn_W4).T, "b4": np.asarray(L0_gnn_b4),
        "gate_w": np.asarray(L0_ffn_gate_W), "gate_b": np.asarray(L0_ffn_gate_b),
        "expert_w": np.asarray(L0_ffn_expert_W), "expert_b": np.asarray(L0_ffn_expert_b),
        "ident": np.eye(P, dtype=np.float32),
        "head_pick": head_pick.reshape(96, H * P),
        "before": np.tril(np.ones((E, E), np.float32), -1).reshape(-1),
    }
    nc = bacc.Bacc("TRN2", target_bir_lowering=False, num_devices=1)
    feeds, aps = {}, []
    for name, a in arrays.items():
        a = np.ascontiguousarray(a)
        feeds["in_" + name] = a
        aps.append(nc.dram_tensor("in_" + name, a.shape, mybir.dt.from_np(a.dtype), kind="ExternalInput").ap())
    aps.append(nc.dram_tensor("out_x", (N, F), F32, kind="ExternalOutput").ap())
    layer_kernel(nc, *aps)
    r = run_bass_kernel_spmd(nc, [feeds], core_ids=[0])
    return r.results[0]["out_x"]
```

```python
from contextlib import ExitStack

import concourse.bass as bass
from concourse import mybir

ALU = mybir.AluOpType
ACT = mybir.ActivationFunctionType
AX = mybir.AxisListType
F32 = mybir.dt.float32
F32R = mybir.dt.float32r
BF16 = mybir.dt.bfloat16
RMAX = bass.bass_isa.ReduceOp.max

P = 128
N = 2048
F = 512
H = 8
D = 64
DX = D + 1
NT = N // P
KF = F // P
CH = 512
NC = N // CH
TC = CH // P
E = 8
PARTS = 3
JG = 4
NG = NT // JG
F1, F2, F3 = 256, 128, 256
ALPHA = 0.2
LN_EPS = 1e-5
GATE_EPS = 1e-4
W_THRES = 0.1
TOPK = 2
STEEP = float(2 ** 64)


def layer_kernel(nc, x, adj_t, w, a1, a2, w1, b1, w2, b2, w3, b3, w4, b4,
                 gate_w, gate_b, expert_w, expert_b, ident, head_pick, before, out):
    with ExitStack() as whole:
        def sb(stack, name, shape, dt=F32):
            return stack.enter_context(nc.sbuf_tensor(name, shape, dt))

        def ps(stack, name, shape, dt=F32):
            return stack.enter_context(nc.psum_tensor(name, shape, dt))

        def sem(name):
            return whole.enter_context(nc.semaphore(name))

        carried = sem("carried")
        id_sb = sb(whole, "id_sb", [P, P])
        x_tiles = x.rearrange("(t p) f -> p t f", p=P)
        out_tiles = out.rearrange("(t p) f -> p t f", p=P)
        adj_tiles = adj_t.rearrange("(t p) i -> p t i", p=P)

        num = sb(whole, "num", [P, NT, H, DX])
        colsum = sb(whole, "colsum", [P, H, DX])

        attention = ExitStack()
        scale = sb(attention, "scale", [P, NT, H, 2])
        adj_bf = sb(attention, "adj_bf", [P, 2, NT, CH], BF16)
        steep_d = sb(attention, "steep_d", [P, NT, H])
        s_rows3 = sb(attention, "s_rows3", [96, N], BF16)
        pick = sb(attention, "pick", [96, H + 1, P], BF16)
        adj_in = sb(attention, "adj_in", [P, 2, CH])

        rows = adj_bf[0:2 * H, 1].rearrange("p t i -> p (t i)").bitcast(F32)[:, 0:N]
        with ExitStack() as st:
            xs = sb(st, "xs", [P, NT, F])
            xt_hi = sb(st, "xt_hi", [P, 2, KF, CH], F32R)
            xt_lo = sb(st, "xt_lo", [P, 2, KF, CH], F32R)
            xn = sb(st, "xn", [P, TC, F])
            adj_in2 = sb(st, "adj_in2", [P, 2, CH])
            w_raw = sb(st, "w_raw", [P, KF, F])
            w_hi = sb(st, "w_hi", [P, KF, F], F32R)
            w_lo = sb(st, "w_lo", [P, KF, F], F32R)
            a_in = sb(st, "a_in", [P, 2, F])
            wa_prod = sb(st, "wa_prod", [P, KF, F])
            wa = sb(st, "wa", [P, KF, 2 * H])
            wa_hi = sb(st, "wa_hi", [P, KF, 2 * H], F32R)
            wa_lo = sb(st, "wa_lo", [P, KF, 2 * H], F32R)
            stats = sb(st, "stats", [P, TC, 6])
            mv = sb(st, "mv", [P, TC, 2])
            rstd = sb(st, "rstd", [P, TC])
            half = sb(st, "half", [P, TC])
            eps = sb(st, "eps", [P, TC])
            p_x = ps(st, "p_x", [P, KF, CH])
            p_wh = ps(st, "p_wh", [P, 2, F])
            p_rows = ps(st, "p_rows", [2 * H, CH])

            id_in, w_in, a_in_s = sem("id_in"), sem("w_in"), sem("a_in_s")
            x_in = [sem("x_in0"), sem("x_in1")]
            a0_in, a0_read = [sem("a0_in0"), sem("a0_in1")], sem("a0_read")
            whi_done, wlo_done, wa_step, wa_cut = sem("whi_done"), sem("wlo_done"), sem("wa_step"), sem("wa_cut")
            half_done, var_done, mean_done, rstd_done, xn_done = (
                sem("half_done"), sem("var_done"), sem("mean_done"), sem("rstd_done"), sem("xn_done"))
            xt_done, xhi_done, xlo_done = sem("xt_done"), sem("xhi_done"), sem("xlo_done")
            wh_done, wh_out, rows_done, rows_out = sem("wh_done"), sem("wh_out"), sem("rows_done"), sem("rows_out")
            ones_done = sem("ones_done")

            with nc.Block() as block:
                @block.sync
                def _(sp):
                    for g in range(2):
                        sp.dma_start(xs[:, g * TC:(g + 1) * TC, :], x_tiles[:, g * TC:(g + 1) * TC, :]).then_inc(x_in[g], 16)
                    sp.dma_start(id_sb[:], ident).then_inc(id_in, 16)
                    sp.dma_start(w_raw[:], w.rearrange("(k p) c -> p k c", p=P)).then_inc(w_in, 16)
                    sp.dma_start(a_in[:, 0, :], a1.partition_broadcast(P)).then_inc(a_in_s, 16)
                    sp.dma_start(a_in[:, 1, :], a2.partition_broadcast(P)).then_inc(a_in_s, 16)
                    for g in range(2, NC):
                        sp.wait_ge(x_in[g % 2], 16)
                        sp.dma_start(xs[:, g * TC:(g + 1) * TC, :], x_tiles[:, g * TC:(g + 1) * TC, :]).then_inc(x_in[g % 2], 16)
                    for j in range(NT // 2):
                        if j >= 2:
                            sp.wait_ge(a0_read, j - 1)
                        sp.dma_start((adj_in, adj_in2)[j % 2][:], adj_tiles[:, j * 2:(j + 1) * 2, 0:CH]).then_inc(a0_in[j % 2], 16)

                @block.gpsimd
                def _(pool):
                    pool.memset(half[:], -0.5).then_inc(half_done, 1)
                    pool.memset(eps[:], LN_EPS).then_inc(half_done, 1)
                    pool.memset(num[:, :, :, D:DX], 1.0).then_inc(ones_done, 1)
                    pool.memset(colsum[:, :, D:DX], float(N)).then_inc(ones_done, 1)
                    pool.wait_ge(half_done, 2)

                    def group(k):
                        pool.wait_ge(mean_done, TC * (k + 1))
                        pool.tensor_tensor(rstd[:], mv[:, :, 1], eps[:], ALU.add).then_inc(var_done, 1)
                        pool.wait_ge(var_done, k + 1)
                        pool.tensor_tensor(rstd[:], rstd[:], half[:], ALU.pow).then_inc(rstd_done, 1)

                    with pool.Fori(0, NC) as k:
                        group(k)
                    for j in range(NT // 2):
                        pool.wait_ge(a0_in[j % 2], 16 * (j // 2 + 1))
                        pool.tensor_scalar(adj_bf[:, 0, j * 2:(j + 1) * 2, :], (adj_in, adj_in2)[j % 2][:], 0.0, None, ALU.is_gt).then_inc(a0_read, 1)

                @block.vector
                def _(dve):
                    def group(gg, b):
                        k = gg * 2 + b
                        dve.wait_ge(x_in[b], 16 * (gg + 1))
                        dve.sem_inc(carried, 1)
                        for u in range(TC):
                            dve.bn_stats(stats[:, u, :], xs[:, bass.ds(k * TC + u, 1), :].rearrange("p a f -> p (a f)")).then_inc(wa_step, 1)
                        for u in range(TC):
                            dve.wait_ge(wa_step, k * TC + u + 5)
                            dve.sem_inc(carried, 1)
                            dve.bn_aggr(mv[:, u, :], stats[:, u, :]).then_inc(mean_done, 1)
                        dve.wait_ge(rstd_done, k + 1)
                        for u in range(TC):
                            xv = xs[:, bass.ds(k * TC + u, 1), :].rearrange("p a f -> p (a f)")
                            dve.tensor_scalar(xn[:, u, :], xv, mv[:, u, 0:1], rstd[:, u:u + 1], ALU.subtract, ALU.mult).then_inc(xn_done, 1)
                        for f in range(KF):
                            dve.wait_ge(xhi_done, k * KF + f + 1)
                            dve.tensor_tensor(xt_lo[:, b, f, :], p_x[:, f, :], xt_hi[:, b, f, :].bitcast(F32),
                                              ALU.subtract).then_inc(xlo_done, 1)

                    dve.wait_ge(w_in, 16)
                    dve.wait_ge(a_in_s, 32)
                    for i in range(2):
                        if i:
                            dve.wait_ge(wa_step, 2)
                        dve.tensor_tensor(wa_prod[:], w_raw[:], a_in[:, i:i + 1, :].broadcast_to([P, KF, F]),
                                          ALU.mult).then_inc(wa_step, 1)
                        dve.wait_ge(wa_step, 2 * i + 1)
                        dve.tensor_reduce(wa[:, :, i * H:(i + 1) * H], wa_prod[:].rearrange("p k (h d) -> p k h d", h=H),
                                          AX.X, ALU.add).then_inc(wa_step, 1)
                    dve.wait_ge(whi_done, 1)
                    dve.tensor_tensor(w_lo[:], w_raw[:], w_hi[:].bitcast(F32), ALU.subtract).then_inc(wlo_done, 1)
                    dve.wait_ge(wa_step, 4)
                    dve.tensor_copy(wa_hi[:], wa[:]).then_inc(wa_cut, 1)
                    dve.wait_ge(wa_cut, 1)
                    dve.tensor_tensor(wa_lo[:], wa[:], wa_hi[:].bitcast(F32), ALU.subtract).then_inc(wa_cut, 1)
                    with dve.Fori(0, NC // 2) as gg:
                        for b in range(2):
                            group(gg, b)

                @block.scalar
                def _(act):
                    act.wait_ge(w_in, 16)
                    act.activation(w_hi[:], w_raw[:], ACT.Copy).then_inc(whi_done, 1)

                    def group(gg, b):
                        k = gg * 2 + b
                        for f in range(KF):
                            act.wait_ge(xt_done, k * KF + f + 1)
                            act.activation(xt_hi[:, b, f, :], p_x[:, f, :], ACT.Copy).then_inc(xhi_done, 1)
                        act.wait_ge(rows_done, k + 1)
                        act.activation(rows[:, bass.ds(k * CH, CH)], p_rows[:], ACT.Copy).then_inc(rows_out, 1)
                        for u in range(TC):
                            act.wait_ge(wh_done, k * TC + u + 1)
                            act.activation(num[:, bass.ds(k * TC + u, 1), :, 0:D].rearrange("p a h d -> p (a h) d"),
                                           p_wh[:, u % 2, :].rearrange("p (h d) -> p h d", h=H), ACT.Copy).then_inc(wh_out, 1)

                    with act.Fori(0, NC // 2) as gg:
                        for b in range(2):
                            group(gg, b)

                @block.tensor
                def _(pe):
                    pe.wait_ge(id_in, 16)

                    def turn(k):
                        for u in range(TC):
                            pe.wait_ge(xn_done, k * TC + u + 1)
                            for f in range(KF):
                                mm = pe.transpose(p_x[:, f, u * P:(u + 1) * P],
                                                  xn[:, u, f * P:(f + 1) * P], id_sb[:])
                                if u == TC - 1:
                                    mm.then_inc(xt_done, 1)

                    def products(k, b, first):
                        pe.wait_ge(xlo_done, (k + 1) * KF)
                        if not first:
                            pe.wait_ge(rows_out, k)
                        for n, (l, r) in enumerate([(wa_hi, xt_hi), (wa_hi, xt_lo), (wa_lo, xt_hi)]):
                            for f in range(KF):
                                mm = pe.matmul(p_rows[:], l[:, f, :], r[:, b, f, :], start=(n + f == 0), stop=(n == 2 and f == KF - 1))
                        mm.then_inc(rows_done, 1)
                        for u in range(TC):
                            if not (first and u < 2):
                                pe.wait_ge(wh_out, k * TC + u - 1)
                            for f in range(KF):
                                hi, lo = (t[:, b, f, u * P:(u + 1) * P] for t in (xt_hi, xt_lo))
                                pe.matmul(p_wh[:, u % 2, :], hi, w_hi[:, f, :], start=(f == 0), stop=False)
                                pe.matmul(p_wh[:, u % 2, :], hi, w_lo[:, f, :], start=False, stop=False)
                                mm = pe.matmul(p_wh[:, u % 2, :], lo, w_hi[:, f, :], start=False, stop=(f == KF - 1))
                            mm.then_inc(wh_done, 1)

                    turn(0)
                    pe.wait_ge(wlo_done, 1)
                    pe.wait_ge(wa_cut, 2)
                    products(0, 0, True)
                    pe.wait_ge(xlo_done, KF)
                    turn(1)
                    products(1, 1, False)
                    with pe.Fori(1, NC // 2) as gg:
                        for b in range(2):
                            turn(gg * 2 + b)
                            products(gg * 2 + b, b, False)

        uv = sb(attention, "uv", [P, NT, H, 2, PARTS, DX], BF16)
        with ExitStack() as st:
            sd = sb(st, "sd", [P, NT, 2 * H])
            dmax = sb(st, "dmax", [P, H])
            dtop = sb(st, "dtop", [P, H])
            ex = sb(st, "ex", [P, 2, NT, H])
            q = sb(st, "q", [P, NT, H])
            m = sb(st, "m", [P, NT, H])
            arg = sb(st, "arg", [P, NT, H, 2])
            ones = sb(st, "ones", [P, P])
            part2 = sb(st, "part2", [H, N], BF16)
            pick_in = sb(st, "pick_in", [96, (H + 1) * P])
            wgt = sb(st, "wgt", [P, 2, 2, H, DX])
            p_sd = ps(st, "p_sd", [P, NT, 2 * H])
            p_cs = ps(st, "p_cs", [P, F])
            sd_done, sd_out, dmax_done, dtop_done = sem("sd_done"), sem("sd_out"), sem("dmax_done"), sem("dtop_done")
            arg_done, m_step, ex_done, scale_done = sem("arg_done"), sem("m_step"), sem("ex_done"), sem("scale_done")
            rest_s, p1_s, p2_s, zero_s, pick_s, pickb_s = (sem("rest_s"), sem("p1_s"), sem("p2_s"), sem("zero_s"),
                                                          sem("pick_s"), sem("pickb_s"))
            shift_s = sem("shift_s")
            ones_s, cs_done, cs_out = sem("ones_s"), sem("cs_done"), sem("cs_out")
            wgt_done, cut1, rest1, cut2, cut3 = sem("wgt_done"), sem("cut1"), sem("rest1"), sem("cut2"), sem("cut3")
            with nc.Block() as block:
                @block.sync
                def _(sp):
                    sp.dma_start(pick_in[:], head_pick).then_inc(pick_s, 16)
                    sp.wait_ge(p1_s, 1)
                    sp.dma_start(s_rows3[H:H + 1, 0:N - CH], s_rows3[0:1, CH:N]).then_inc(shift_s, 16)
                    sp.wait_ge(p2_s, 1)
                    sp.dma_start(s_rows3[32 + H:33 + H, 0:N - CH], s_rows3[32:33, CH:N]).then_inc(shift_s, 16)
                    sp.wait_ge(rest_s, 4)
                    sp.dma_start(s_rows3[64 + H:65 + H, 0:N - CH], s_rows3[64:65, CH:N]).then_inc(shift_s, 16)
                    sp.wait_ge(shift_s, 48)

                @block.tensor
                def _(pe):
                    for t in range(NT):
                        mm = pe.transpose(p_sd[:, t, :], rows[:, t * P:(t + 1) * P], id_sb[0:2 * H, 0:2 * H])
                    mm.then_inc(sd_done, 1)
                    pe.wait_ge(ones_s, 1)
                    for t in range(NT):
                        mm = pe.matmul(p_cs[:], ones[:], num[:, t, :, 0:D], start=(t == 0), stop=(t == NT - 1))
                    mm.then_inc(cs_done, 1)

                @block.vector
                def _(dve):
                    dve.memset(ones[:], 1.0).then_inc(ones_s, 1)
                    dve.memzero(s_rows3[:].bitcast(mybir.dt.uint32)).then_inc(zero_s, 1)
                    dve.wait_ge(sd_done, 1)
                    dve.tensor_copy(sd[:], p_sd[:]).then_inc(sd_out, 1)
                    dve.wait_ge(sd_out, 1)
                    dve.tensor_reduce(dmax[:], sd[:, :, H:2 * H].rearrange("p t h -> p h t"), AX.X, ALU.max).then_inc(dmax_done, 1)
                    dve.tensor_scalar(steep_d[:], sd[:, :, H:2 * H], STEEP, None, ALU.mult).then_inc(m_step, 1)
                    dve.wait_ge(dtop_done, 1)
                    top = dtop[:].rearrange("p (a h) -> p a h", a=1).broadcast_to([P, NT, H])
                    dve.tensor_tensor(ex[:, 0], sd[:, :, H:2 * H], top, ALU.subtract).then_inc(arg_done, 1)
                    dve.tensor_tensor(q[:], sd[:, :, 0:H], top, ALU.add).then_inc(m_step, 1)
                    dve.wait_ge(m_step, 2)
                    dve.scalar_tensor_tensor(m[:], q[:], ALPHA, q[:], ALU.mult, ALU.max).then_inc(m_step, 1)
                    dve.wait_ge(m_step, 3)
                    dve.tensor_tensor(arg[:, :, :, 0], q[:], m[:], ALU.subtract).then_inc(m_step, 1)
                    dve.scalar_tensor_tensor(arg[:, :, :, 1], q[:], ALPHA, m[:], ALU.mult, ALU.subtract).then_inc(m_step, 1)

                    dve.sem_inc(rest1, 2)
                    dve.sem_inc(cut3, 2)
                    with dve.Fori(0, NT) as t:
                        for s in range(2):
                            dve.wait_ge(cut1, 2 * t + s + 1)
                            dve.wait_ge(cut3, 2 * t + s + 1)
                            first = uv[:, bass.ds(t, 1), :, s, 0, :].rearrange("p a h d -> p (a h) d")
                            dve.tensor_tensor(wgt[:, 1, s], wgt[:, 0, s], first, ALU.subtract).then_inc(rest1, 1)
                        for s in range(2):
                            dve.wait_ge(cut2, 2 * t + s + 1)
                            second, third = (uv[:, bass.ds(t, 1), :, s, i, :].rearrange("p a h d -> p (a h) d") for i in (1, 2))
                            dve.tensor_tensor(third, wgt[:, 1, s], second, ALU.subtract).then_inc(cut3, 1)

                    dve.wait_ge(p1_s, 1)
                    dve.tensor_tensor(rows[0:H, :], rows[0:H, :], s_rows3[0:H, :], ALU.subtract).then_inc(rest_s, 1)
                    dve.wait_ge(rest_s, 1)
                    dve.tensor_copy(part2[:], rows[0:H, :]).then_inc(rest_s, 1)
                    dve.wait_ge(rest_s, 2)
                    dve.tensor_tensor(rows[0:H, :], rows[0:H, :], part2[:], ALU.subtract).then_inc(rest_s, 1)
                    dve.wait_ge(rest_s, 3)
                    dve.tensor_copy(s_rows3[64:64 + H, :], rows[0:H, :]).then_inc(rest_s, 1)
                    dve.wait_ge(cs_done, 1)
                    dve.tensor_copy(colsum[:, :, 0:D], p_cs[:].rearrange("p (h d) -> p h d", h=H)).then_inc(cs_out, 1)

                @block.gpsimd
                def _(pool):
                    pool.wait_ge(dmax_done, 1)
                    pool.partition_all_reduce(dtop[:], dmax[:], P, RMAX).then_inc(dtop_done, 1)
                    pool.wait_ge(ex_done, 2)
                    with pool.Fori(0, NT) as t:
                        for s in range(2):
                            pool.wait_ge(rest1, 2 * t + s + 1)
                            pool.tensor_tensor(wgt[:, 0, s], num[:, bass.ds(t, 1), :, :].rearrange("p a h d -> p (a h) d"),
                                               ex[:, s, bass.ds(t, 1), :].rearrange("p a h -> p (a h)").unsqueeze(2).broadcast_to([P, H, DX]),
                                               ALU.mult).then_inc(wgt_done, 1)

                @block.scalar
                def _(act):
                    act.wait_ge(zero_s, 1)
                    act.activation(s_rows3[0:H, :], rows[0:H, :], ACT.Copy).then_inc(p1_s, 1)
                    act.wait_ge(arg_done, 1)
                    act.activation(ex[:, 1], ex[:, 0], ACT.Exp, scale=ALPHA).then_inc(ex_done, 1)
                    act.wait_ge(ex_done, 1)
                    act.activation(ex[:, 0], ex[:, 0], ACT.Exp).then_inc(ex_done, 1)
                    act.wait_ge(m_step, 5)
                    act.activation(scale[:], arg[:], ACT.Exp).then_inc(scale_done, 1)
                    with act.Fori(0, NT) as t:
                        for s in range(2):
                            act.wait_ge(wgt_done, 2 * t + s + 1)
                            act.activation(uv[:, bass.ds(t, 1), :, s, 0, :].rearrange("p a h d -> p (a h) d"),
                                           wgt[:, 0, s], ACT.Copy).then_inc(cut1, 1)
                        for s in range(2):
                            act.wait_ge(rest1, 2 * t + s + 3)
                            act.activation(uv[:, bass.ds(t, 1), :, s, 1, :].rearrange("p a h d -> p (a h) d"),
                                           wgt[:, 1, s], ACT.Copy).then_inc(cut2, 1)
                    act.wait_ge(pick_s, 16)
                    act.activation(pick[:], pick_in[:].rearrange("p (h c) -> p h c", h=H), ACT.Copy).then_inc(pickb_s, 1)
                    act.wait_ge(rest_s, 2)
                    act.activation(s_rows3[32:32 + H, :], part2[:], ACT.Copy).then_inc(p2_s, 1)


        RB = 2
        HT = NG * TC
        with ExitStack() as st:
            m1 = sb(st, "m1", [P, NG, JG, CH], BF16)
            m0 = sb(st, "m0", [P, RB, JG, CH], BF16)
            sums = sb(st, "sums", [P, 2, TC, 2, DX])
            fill = sb(st, "fill", [P, CH], BF16)
            empty = sb(st, "empty", [P, TC])
            mean = sb(st, "mean", [P, TC, DX])
            p_acc = ps(st, "p_acc", [P, TC, CH])
            p_s = ps(st, "p_s", [P, 2, CH])
            adj_in_s, conv_done = sem("adj_in_s"), sem("conv_done")
            s_ready, relu_done, m1_ready, m1_used, m0_ready = (
                sem("s_ready"), sem("relu_done"), sem("m1_ready"), sem("m1_used"), sem("m0_ready"))
            tiles_done, acc_read, sums_used, scaled, fill_s = (
                sem("tiles_done"), sem("acc_read"), sem("sums_used"), sem("scaled"), sem("fill_s"))
            DXX = 2 * PARTS * DX

            def heads(eng, body):
                with eng.Fori(0, NC // 2) as cc:
                    for cb in range(2):
                        with eng.Fori(0, H // 2) as hh:
                            for hb in range(2):
                                body((cc * 2 + cb) * H + hh * 2 + hb, cc * 2 + cb, hh * 2 + hb, hb, cb)

            with nc.Block() as block:
                @block.sync
                def _(sp):
                    for c in range(1, NC):
                        with sp.Fori(0, NT // 2) as j:
                            sp.wait_ge(conv_done, (c - 1) * (NT // 2) + 1 + j)
                            sp.dma_start(adj_in[:], adj_tiles[:, bass.ds(j * 2, 2), c * CH:(c + 1) * CH]).then_inc(adj_in_s, 16)

                @block.gpsimd
                def _(pool):
                    pool.sem_inc(conv_done, 1)
                    pool.sem_inc(sums_used, 3)

                    def scale_head(n, c, h, hb):
                        pool.wait_ge(acc_read, TC * n + 2 * TC)
                        pool.tensor_tensor(sums[:, hb], sums[:, hb],
                                           scale[:, c * TC:(c + 1) * TC, h, :].unsqueeze(3).broadcast_to([P, TC, 2, DX]),
                                           ALU.mult).then_inc(scaled, 1)
                        mine = num[:, c * TC:(c + 1) * TC, h, :]
                        pool.wait_ge(scaled, 4 * n + 1)
                        pool.tensor_tensor(mine, sums[:, hb, :, 0, :], sums[:, hb, :, 1, :], ALU.add).then_inc(sums_used, 1)
                        pool.wait_ge(sums_used, n + 4)
                        pool.tensor_scalar(empty[:], num[:, c * TC:(c + 1) * TC, h, D], 0.0, None, ALU.is_equal).then_inc(scaled, 1)
                        pool.wait_ge(scaled, 4 * n + 2)
                        pool.tensor_tensor(mean[:], colsum[:, h:h + 1, :].broadcast_to([P, TC, DX]),
                                           empty[:].unsqueeze(2).broadcast_to([P, TC, DX]), ALU.mult).then_inc(scaled, 1)
                        pool.wait_ge(scaled, 4 * n + 3)
                        pool.tensor_tensor(mine, mine, mean[:], ALU.add).then_inc(scaled, 1)

                    for c in range(NC):
                        if c >= 1 and c < NC - 1:
                            pool.wait_ge(m0_ready, c * H * NG + NG)
                        for h in range(H):
                            if c < NC - 1:
                                pool.wait_ge(adj_in_s, (c * H + 1 + h) * 16)
                                pool.tensor_scalar(adj_bf[:, (c + 1) % 2, h * 2:(h + 1) * 2, :], adj_in[:], 0.0, None,
                                                   ALU.is_gt).then_inc(conv_done, 1)
                            scale_head(h + c * H, c, h, h % 2)

                @block.scalar
                def _(act):
                    act.sem_inc(relu_done, 2 * NG * JG)

                    def body(n, c, h, hb, cb):
                        act.wait_ge(s_ready, n + 1)
                        for g in range(NG):
                            act.wait_ge(m1_used, n * NG + g + 1)
                            act.wait_ge(m0_ready, n * NG + g + 1)
                            for j in range(JG):
                                t = g * JG + j
                                act.activation(m1[:, g, j, :], p_s[:, hb, :], ACT.Relu, scale=STEEP,
                                               bias=steep_d[:, t, bass.ds(h, 1)]).then_inc(relu_done, 1)

                    heads(act, body)

                @block.vector
                def _(dve):
                    dve.sem_inc(m0_ready, NG)
                    dve.memset(fill[:], 0.0).then_inc(fill_s, 1)

                    def evacuate(n, hb):
                        dve.wait_ge(sums_used, n + 1)
                        for i in range(TC):
                            dve.wait_ge(tiles_done, n * HT + TC + i + 1)
                            dve.tensor_reduce(sums[:, 1 - hb, i], p_acc[:, i, 0:DXX].rearrange("p (m k d) -> p m d k", m=2, k=PARTS),
                                              AX.X, ALU.add).then_inc(acc_read, 1)

                    def body(n, c, h, hb, cb):
                        dve.wait_ge(conv_done, c * (NT // 2) + 1)
                        for g in range(NG):
                            edges = adj_bf[:, cb, g * JG:(g + 1) * JG, :]
                            dve.wait_ge(relu_done, (n * NG + g) * JG + (2 * NG + 1) * JG)
                            dve.tensor_tensor(m1[:, g], m1[:, g], edges, ALU.min).then_inc(m1_ready, 1)
                            dve.wait_ge(tiles_done, (n * NG + g) * TC + TC)
                            dve.wait_ge(m1_ready, n * NG + g + 1)
                            dve.tensor_tensor(m0[:, g % RB], edges, m1[:, g], ALU.subtract).then_inc(m0_ready, 1)
                            if g == 0:
                                evacuate(n, hb)

                    heads(dve, body)
                    evacuate(NC * H, 0)

                @block.tensor
                def _(pe):
                    pe.sem_inc(m1_used, NG)
                    pe.sem_inc(tiles_done, TC)
                    pe.wait_ge(fill_s, 1)
                    for i in range(TC):
                        pe.matmul(p_acc[:, i, :], fill[:, 0:P], fill[:], start=True, stop=True).then_inc(tiles_done, 1)

                    pe.matmul(p_s[:, 0, :], pick[:, 0, :], s_rows3[:, 0:CH], start=True, stop=True).then_inc(s_ready, 1)

                    def body(n, c, h, hb, cb):
                        for g in range(NG):
                            if g == 1:
                                pe.wait_ge(relu_done, n * NG * JG + 2 * NG * JG)
                                pe.matmul(p_s[:, 1 - hb, :], pick[:, bass.ds(h + 1, 1), :].rearrange("p a c -> p (a c)"),
                                          s_rows3[:, bass.ds(c * CH, CH)], start=True, stop=True).then_inc(s_ready, 1)
                            pe.wait_ge(m1_ready, n * NG + g + 1)
                            for i in range(TC):
                                if g == 0:
                                    pe.wait_ge(acc_read, n * TC + i + 1)
                                for j in range(JG):
                                    mm = pe.matmul(p_acc[:, i, 0:DXX // 2], m1[:, g, j, i * P:(i + 1) * P],
                                                   uv[:, g * JG + j, bass.ds(h, 1), 0].rearrange("p a k d -> p (a k d)"),
                                                   start=(g == 0 and j == 0), stop=False, skip_group_check=True)
                            mm.then_inc(m1_used, 1)
                            pe.wait_ge(m0_ready, n * NG + g + 1 + NG)
                            for i in range(TC):
                                for j in range(JG):
                                    mm = pe.matmul(p_acc[:, i, DXX // 2:DXX], m0[:, g % RB, j, i * P:(i + 1) * P],
                                                   uv[:, g * JG + j, bass.ds(h, 1), 1].rearrange("p a k d -> p (a k d)"),
                                                   start=False, stop=(g == NG - 1 and j == JG - 1), skip_group_check=True)
                                mm.then_inc(tiles_done, 1)

                    heads(pe, body)
        attention.close()

        late = ExitStack()
        x2 = sb(late, "x2", [P, NT, F])
        x2t_hi = sb(late, "x2t_hi", [P, KF, N], F32R)
        x2t_lo = sb(late, "x2t_lo", [P, KF, N], F32R)
        g_rows = sb(late, "g_rows", [E, N])
        with ExitStack() as st:
            layers = [("w1", w1, F, F1), ("w2", w2, F1, F2), ("w3", w3, F2, F3), ("w4", w4, F3, F), ("gate", gate_w, F, E)]
            cut = {}
            for name, src, k, m_ in layers:
                cut[name] = (sb(st, name + "_hi", [P, k // P, m_], F32R), sb(st, name + "_lo", [P, k // P, m_], F32R))
            b1_sb, b2_sb, b3_sb = sb(st, "b1_sb", [P, F1 // P]), sb(st, "b2_sb", [P, F2 // P]), sb(st, "b3_sb", [P, F3 // P])
            b4_sb = sb(st, "b4_sb", [P, F])
            h_sb = sb(st, "h_sb", [P, TC, F])
            e_sb = sb(st, "e_sb", [P, TC, F])
            et_hi = sb(st, "et_hi", [P, KF, CH], F32R)
            et_lo = sb(st, "et_lo", [P, KF, CH], F32R)
            y_f = sb(st, "y_f", [P, 2, CH])
            y_hi = sb(st, "y_hi", [P, 2, CH], F32R)
            y_lo = sb(st, "y_lo", [P, 2, CH], F32R)
            rden = sb(st, "rden", [P, TC, H])
            stats = sb(st, "stats2", [P, TC, 6])
            mv = sb(st, "mv2", [P, TC, 2])
            rstd = sb(st, "rstd2", [P, TC])
            half = sb(st, "half2", [P, TC])
            eps = sb(st, "eps2", [P, TC])
            p_t = ps(st, "p_t", [P, KF, CH])
            p_m = ps(st, "p_m", [P, 4, CH])
            raw_in = [sem(f"raw_in{i}") for i in range(5)]
            b_in, raw_hi, raw_lo = sem("b_in"), sem("raw_hi"), sem("raw_lo")
            xb_in = [sem(f"xb_in{c}") for c in range(NC)]
            half_s, h_step, exp_s = sem("half_s"), sem("h_step"), sem("exp_s")
            turned, e_hi, e_lo = sem("turned"), sem("e_hi"), sem("e_lo")
            mm_done, y_act, y_cut = sem("mm_done"), sem("y_act"), sem("y_cut")
            xb_s, x2_s, stat_s, mean_s, var_s, rstd_s = (
                sem("xb_s"), sem("x2_s"), sem("stat_s"), sem("mean_s"), sem("var_s"), sem("rstd_s"))
            xn2_s, turned2, n_hi, n_lo, g_done, g_out = (
                sem("xn2_s"), sem("turned2"), sem("n_hi"), sem("n_lo"), sem("g_done"), sem("g_out"))

            raw, at = {}, 0
            flat = x2[:].rearrange("p t f -> p (t f)")
            for name, src, k, m_ in layers:
                raw[name] = flat[:, at:at + k // P * m_].rearrange("p (k m) -> p k m", m=m_)
                at += k // P * m_

            def spare(c):
                return num[:, c * TC:(c + 1) * TC].rearrange("p t h d -> p (t h d)")[:, 0:TC * F].rearrange("p (t f) -> p t f", f=F)

            def steps(stage_parts):
                for k in range(NC + 2):
                    for lag, part in stage_parts:
                        if 0 <= k - lag < NC:
                            part(k - lag)

            with nc.Block() as block:
                @block.sync
                def _(sp):
                    for i, (name, src, k, m_) in enumerate(layers):
                        sp.dma_start(raw[name], src.rearrange("(k p) m -> p k m", p=P)).then_inc(raw_in[i], 16)
                    for dst, src in ((b1_sb, b1), (b2_sb, b2), (b3_sb, b3)):
                        sp.dma_start(dst[:], src).then_inc(b_in, 16)
                    sp.dma_start(b4_sb[:], b4.partition_broadcast(P)).then_inc(b_in, 16)
                    for c in range(NC):
                        sp.wait_ge(h_step, c * 5 + 2)
                        sp.dma_start(spare(c), x_tiles[:, c * TC:(c + 1) * TC, :]).then_inc(xb_in[c], 16)

                @block.gpsimd
                def _(pool):
                    pool.memset(half[:], -0.5).then_inc(half_s, 1)
                    pool.memset(eps[:], LN_EPS).then_inc(half_s, 1)
                    pool.wait_ge(b_in, 64)
                    pool.wait_ge(half_s, 2)

                    def residual(c):
                        pool.wait_ge(xb_in[c], 16)
                        pool.tensor_tensor(spare(c), spare(c), b4_sb[:].unsqueeze(1).broadcast_to([P, TC, F]), ALU.add).then_inc(xb_s, 1)

                    def deviation(c):
                        pool.wait_ge(mean_s, TC * (c + 1))
                        pool.tensor_tensor(rstd[:], mv[:, :, 1], eps[:], ALU.add).then_inc(var_s, 1)
                        pool.wait_ge(var_s, c + 1)
                        pool.tensor_tensor(rstd[:], rstd[:], half[:], ALU.pow).then_inc(rstd_s, 1)

                    steps([(0, residual), (1, deviation)])

                @block.vector
                def _(dve):
                    for i, (name, src, k, m_) in enumerate(layers):
                        dve.wait_ge(raw_hi, i + 1)
                        dve.tensor_tensor(cut[name][1][:], raw[name], cut[name][0][:].bitcast(F32), ALU.subtract).then_inc(raw_lo, 1)

                    def heads_out(c):
                        mine = num[:, c * TC:(c + 1) * TC]
                        dve.reciprocal(rden[:], mine[:, :, :, D]).then_inc(h_step, 1)
                        dve.wait_ge(h_step, c * 5 + 1)
                        if c:
                            dve.wait_ge(turned, c * KF)
                        dve.tensor_tensor(h_sb[:].rearrange("p t (h d) -> p t h d", h=H), mine[:, :, :, 0:D],
                                          rden[:].unsqueeze(3).broadcast_to([P, TC, H, D]), ALU.mult).then_inc(h_step, 1)
                        dve.wait_ge(h_step, c * 5 + 2)
                        dve.tensor_scalar(e_sb[:], h_sb[:], 0.0, None, ALU.min).then_inc(h_step, 1)

                    def elu(c):
                        dve.wait_ge(exp_s, c + 1)
                        dve.scalar_tensor_tensor(h_sb[:], h_sb[:], 0.0, e_sb[:], ALU.max, ALU.add).then_inc(h_step, 1)
                        dve.wait_ge(h_step, c * 5 + 4)
                        dve.tensor_scalar(h_sb[:], h_sb[:], -1.0, None, ALU.add).then_inc(h_step, 1)

                    def enc_lo(c):
                        for f in range(KF):
                            dve.wait_ge(e_hi, c * KF + f + 1)
                            dve.tensor_tensor(et_lo[:, f, :], p_t[:, f, :], et_hi[:, f, :].bitcast(F32), ALU.subtract).then_inc(e_lo, 1)

                    def hidden_lo(c, first, slots):
                        for n, slot in enumerate(slots, first):
                            dve.wait_ge(y_act, c * 10 + 2 * n + 2)
                            dve.tensor_tensor(y_lo[:, slot, :], y_f[:, slot, :], y_hi[:, slot, :].bitcast(F32), ALU.subtract).then_inc(y_cut, 1)

                    def layer_out(c):
                        dve.wait_ge(xb_s, c + 1)
                        for i in range(TC):
                            dve.wait_ge(mm_done, c * 9 + 6 + i)
                            dve.tensor_tensor(x2[:, c * TC + i, :], p_m[:, i, :], spare(c)[:, i, :], ALU.add).then_inc(x2_s, 1)
                        for i in range(TC):
                            dve.wait_ge(x2_s, c * TC + i + 1)
                            dve.bn_stats(stats[:, i, :], x2[:, c * TC + i, :]).then_inc(stat_s, 1)
                        for i in range(TC):
                            dve.wait_ge(stat_s, c * TC + i + 1)
                            dve.bn_aggr(mv[:, i, :], stats[:, i, :]).then_inc(mean_s, 1)

                    def norm(c):
                        dve.wait_ge(rstd_s, c + 1)
                        for i in range(TC):
                            dve.tensor_scalar(spare(c)[:, i, :], x2[:, c * TC + i, :], mv[:, i, 0:1], rstd[:, i:i + 1],
                                              ALU.subtract, ALU.mult).then_inc(xn2_s, 1)

                    def norm_lo(c):
                        for f in range(KF):
                            dve.wait_ge(n_hi, c * KF + f + 1)
                            here = (slice(None), f, slice(c * CH, (c + 1) * CH))
                            dve.tensor_tensor(x2t_lo[here], p_t[:, f, :], x2t_hi[here].bitcast(F32), ALU.subtract).then_inc(n_lo, 1)

                    steps([(0, heads_out), (2, norm), (1, lambda c: hidden_lo(c, 0, (0, 1))), (2, norm_lo),
                           (1, lambda c: hidden_lo(c, 2, (0,))), (0, elu), (1, lambda c: hidden_lo(c, 3, (0, 1))),
                           (0, enc_lo), (1, layer_out)])

                @block.scalar
                def _(act):
                    for i, (name, src, k, m_) in enumerate(layers):
                        act.wait_ge(raw_in[i], 16)
                        act.activation(cut[name][0][:], raw[name], ACT.Copy).then_inc(raw_hi, 1)
                    act.wait_ge(b_in, 64)

                    def exp(c):
                        act.wait_ge(h_step, c * 5 + 3)
                        act.activation(e_sb[:], e_sb[:], ACT.Exp).then_inc(exp_s, 1)

                    def enc_hi(c):
                        for f in range(KF):
                            act.wait_ge(turned, c * KF + f + 1)
                            act.activation(et_hi[:, f, :], p_t[:, f, :], ACT.Copy).then_inc(e_hi, 1)

                    hidden = [(0, b1_sb[:, 0:1], 0), (1, b1_sb[:, 1:2], 1), (2, b2_sb[:, 0:1], 0),
                              (0, b3_sb[:, 0:1], 0), (1, b3_sb[:, 1:2], 1)]

                    def relu(c, which):
                        for n in which:
                            bank, bias, slot = hidden[n]
                            act.wait_ge(mm_done, c * 9 + (5 if n == 3 else n + 1))
                            act.activation(y_f[:, slot, :], p_m[:, bank, :], ACT.Relu, bias=bias).then_inc(y_act, 1)
                            act.activation(y_hi[:, slot, :], p_m[:, bank, :], ACT.Relu, bias=bias).then_inc(y_act, 1)

                    def norm_hi(c):
                        for f in range(KF):
                            act.wait_ge(turned2, c * KF + f + 1)
                            act.activation(x2t_hi[:, f, c * CH:(c + 1) * CH], p_t[:, f, :], ACT.Copy).then_inc(n_hi, 1)

                    def scores(c):
                        act.wait_ge(g_done, c + 1)
                        act.activation(g_rows[:, c * CH:(c + 1) * CH], p_m[0:E, 3, :], ACT.Copy).then_inc(g_out, 1)

                    steps([(0, exp), (1, lambda c: relu(c, (0, 1))), (2, norm_hi), (1, lambda c: relu(c, (2,))),
                           (2, scores), (1, lambda c: relu(c, (3, 4))), (0, enc_hi)])

                @block.tensor
                def _(pe):
                    pe.wait_ge(raw_lo, len(layers))

                    def product(dst, name, o, k, hi, lo):
                        w_h, w_l = cut[name]
                        for n, (l, r) in enumerate([(w_h, hi), (w_l, hi), (w_h, lo)]):
                            for f in range(k):
                                mm = pe.matmul(dst, l[:, f, o * P:(o + 1) * P], r[:, f, :], start=(n + f == 0), stop=(n == 2 and f == k - 1))
                        return mm

                    def turn(src, done):
                        for f in range(KF):
                            for i in range(TC):
                                mm = pe.transpose(p_t[:, f, i * P:(i + 1) * P], src[:, i, f * P:(f + 1) * P], id_sb[:])
                            mm.then_inc(done, 1)

                    def turn_enc(c):
                        pe.wait_ge(h_step, c * 5 + 5)
                        if c >= 2:
                            pe.wait_ge(n_lo, (c - 1) * KF)
                        turn(h_sb, turned)

                    def layer1(c):
                        pe.wait_ge(e_lo, (c + 1) * KF)
                        if c:
                            pe.wait_ge(x2_s, c * TC - 2)
                        for o in range(F1 // P):
                            product(p_m[:, o, :], "w1", o, KF, et_hi, et_lo).then_inc(mm_done, 1)

                    def layer2(c):
                        pe.wait_ge(y_cut, c * 5 + 2)
                        if c:
                            pe.wait_ge(x2_s, c * TC)
                        product(p_m[:, 2, :], "w2", 0, 2, y_hi, y_lo).then_inc(mm_done, 1)

                    def layer3(c):
                        pe.wait_ge(y_cut, c * 5 + 3)
                        for o in range(F3 // P):
                            product(p_m[:, o, :], "w3", o, 1, y_hi, y_lo).then_inc(mm_done, 1)

                    def layer4(c):
                        pe.wait_ge(y_cut, c * 5 + 5)
                        if c:
                            pe.wait_ge(g_out, c)
                        w_h, w_l = cut["w4"]
                        for i in range(TC):
                            for n, (l, r) in enumerate([(y_hi, w_h), (y_hi, w_l), (y_lo, w_h)]):
                                for f in range(2):
                                    mm = pe.matmul(p_m[:, i, :], l[:, f, i * P:(i + 1) * P], r[:, f, :],
                                                   start=(n + f == 0), stop=(n == 2 and f == 1))
                            mm.then_inc(mm_done, 1)

                    def turn_norm(c):
                        pe.wait_ge(xn2_s, (c + 1) * TC)
                        if c + 1 < NC:
                            pe.wait_ge(e_lo, (c + 2) * KF)
                        turn(spare(c), turned2)

                    def gate(c):
                        pe.wait_ge(n_lo, (c + 1) * KF)
                        w_h, w_l = cut["gate"]
                        at = slice(c * CH, (c + 1) * CH)
                        for n, (l, r) in enumerate([(w_h, x2t_hi), (w_l, x2t_hi), (w_h, x2t_lo)]):
                            for f in range(KF):
                                mm = pe.matmul(p_m[0:E, 3, :], l[:, f, :], r[:, f, at], start=(n + f == 0), stop=(n == 2 and f == KF - 1))
                        mm.then_inc(g_done, 1)

                    steps([(1, layer1), (2, turn_norm), (1, layer2), (2, gate), (1, layer3), (0, turn_enc), (1, layer4)])

        with ExitStack() as st:
            raw_w = sb(st, "raw_w", [P, 2, KF, F])
            ew_hi = sb(st, "ew_hi", [P, 2, KF, F], F32R)
            ew_lo = sb(st, "ew_lo", [P, 2, KF, F], F32R)
            gb_sb = sb(st, "gb_sb", [P, E])
            tri = sb(st, "tri", [P, E * E])
            eb_sb = sb(st, "eb_sb", [E, F])
            sc = sb(st, "sc", [P, NT, E])
            gt = sb(st, "gt", [P, NT, E, E])
            eq = sb(st, "eq", [P, NT, E, E])
            rank = sb(st, "rank", [P, NT, E])
            col = sb(st, "col", [P, 4, NT])
            pr = sb(st, "pr", [P, NT, E])
            comb_t = num[:].rearrange("p t h d -> p (t h d)")[0:E, 0:N]
            p_y = ps(st, "p_y", [P, 4, F])
            p_g = ps(st, "p_g", [P, NT * E])
            gt_s = sem("gt_s")
            p_c = ps(st, "p_c", [E, 3, CH])
            ew_in = [sem("ew_in0"), sem("ew_in1")]
            small_in, ewhi_s, ewlo_s, sc_step, ex2_s = (
                sem("small_in"), sem("ewhi_s"), sem("ewlo_s"), sem("sc_step"), sem("ex2_s"))
            ct_done, ct_out, y_done, y_read, out_s = sem("ct_done"), sem("ct_out"), sem("y_done"), sem("y_read"), sem("out_s")
            RING = 4
            with nc.Block() as block:
                @block.sync
                def _(sp):
                    for dst, src in ((gb_sb[:], gate_b.partition_broadcast(P)), (tri[:], before.partition_broadcast(P)), (eb_sb[:], expert_b)):
                        sp.dma_start(dst, src).then_inc(small_in, 16)
                    ew = expert_w.rearrange("e (k p) f -> e p k f", p=P)
                    with sp.Fori(0, E // 2) as ee:
                        for b in range(2):
                            sp.wait_ge(ewlo_s, ee * 2 + b + 1)
                            sp.dma_start(raw_w[:, b], ew[bass.ds(ee * 2 + b, 1)].rearrange("e p k f -> p (e k) f")).then_inc(ew_in[b], 16)
                    for t in range(NT):
                        sp.wait_ge(y_read, RING + (E) * NT + t + 1)
                        sp.dma_start(out_tiles[:, t, :], x2[:, t, :]).then_inc(out_s, 16)
                    sp.wait_ge(out_s, 16 * NT)

                @block.gpsimd
                def _(pool):
                    pool.sem_inc(ewlo_s, 2)
                    with pool.Fori(0, E // 2) as ee:
                        for b in range(2):
                            pool.wait_ge(ewhi_s, ee * 2 + b + 1)
                            pool.tensor_tensor(ew_lo[:, b], raw_w[:, b], ew_hi[:, b].bitcast(F32), ALU.subtract).then_inc(ewlo_s, 1)

                @block.scalar
                def _(act):
                    def cut_hi(ee, b):
                        act.wait_ge(ew_in[b], 16 * (ee + 1))
                        act.wait_ge(y_done, ee * 2 * NT + b * NT + 2 * NT)
                        act.activation(ew_hi[:, b], raw_w[:, b], ACT.Copy).then_inc(ewhi_s, 1)

                    act.sem_inc(y_done, 3 * NT)
                    for b in range(2):
                        cut_hi(0, b)
                    act.wait_ge(sc_step, 7)
                    act.activation(pr[:], pr[:], ACT.Exp).then_inc(ex2_s, 1)
                    with act.Fori(1, E // 2) as ee:
                        for b in range(2):
                            cut_hi(ee, b)

                @block.vector
                def _(dve):
                    steps = [0]

                    def step(ins):
                        steps[0] += 1
                        ins.then_inc(sc_step, 1)
                        dve.wait_ge(sc_step, steps[0])

                    dve.wait_ge(small_in, 48)
                    dve.wait_ge(gt_s, 1)
                    step(dve.tensor_tensor(sc[:], p_g[:].rearrange("p (t e) -> p t e", e=E), gb_sb[:].unsqueeze(1).broadcast_to([P, NT, E]), ALU.add))
                    step(dve.tensor_scalar(sc[:], sc[:], GATE_EPS, None, ALU.max))
                    other = sc[:].unsqueeze(2).broadcast_to([P, NT, E, E])
                    own = sc[:].unsqueeze(3).broadcast_to([P, NT, E, E])
                    step(dve.tensor_tensor(gt[:], other, own, ALU.is_gt))
                    step(dve.tensor_tensor(eq[:], other, own, ALU.is_equal))
                    ones_before = tri[:].rearrange("p (e f) -> p e f", e=E).unsqueeze(1).broadcast_to([P, NT, E, E])
                    step(dve.tensor_tensor(eq[:], eq[:], ones_before, ALU.mult))
                    step(dve.tensor_reduce(col[:, 0, :], sc[:], AX.X, ALU.max))
                    step(dve.tensor_tensor(pr[:], sc[:], col[:, 0, :].unsqueeze(2).broadcast_to([P, NT, E]), ALU.subtract))
                    step(dve.tensor_tensor(gt[:], gt[:], eq[:], ALU.add))
                    step(dve.tensor_reduce(rank[:], gt[:], AX.X, ALU.add))
                    step(dve.tensor_scalar(rank[:], rank[:], float(TOPK), None, ALU.is_lt))
                    dve.wait_ge(ex2_s, 1)
                    step(dve.tensor_reduce(col[:, 1, :], pr[:], AX.X, ALU.add))
                    step(dve.reciprocal(col[:, 1, :], col[:, 1, :]))
                    step(dve.tensor_tensor(pr[:], pr[:], col[:, 1, :].unsqueeze(2).broadcast_to([P, NT, E]), ALU.mult))
                    step(dve.scalar_tensor_tensor(pr[:], pr[:], W_THRES, rank[:], ALU.max, ALU.mult))
                    step(dve.tensor_reduce(col[:, 2, :], pr[:], AX.X, ALU.add))
                    step(dve.tensor_scalar(col[:, 2, :], col[:, 2, :], float(TOPK), None, ALU.mult))
                    step(dve.reciprocal(col[:, 3, :], col[:, 2, :]))
                    step(dve.tensor_tensor(pr[:], pr[:], col[:, 3, :].unsqueeze(2).broadcast_to([P, NT, E]), ALU.mult))

                    def expert(e, first):
                        for t in range(NT):
                            dve.wait_ge(y_done, e * NT + t + 1 + 3 * NT)
                            if not first:
                                dve.wait_ge(y_read, (e - 1) * NT + t + 1 + RING)
                            dve.scalar_tensor_tensor(x2[:, t, :], p_y[:, t % RING, :], pr[:, t, bass.ds(e, 1)], x2[:, t, :],
                                                     ALU.mult, ALU.add).then_inc(y_read, 1)

                    dve.sem_inc(y_read, RING)
                    expert(0, True)
                    for t4 in range(NC):
                        dve.wait_ge(ct_done, t4 + 1)
                        dve.tensor_copy(comb_t[:, t4 * CH:(t4 + 1) * CH], p_c[:, t4 % 3, :]).then_inc(ct_out, 1)
                    with dve.Fori(1, E) as e:
                        expert(e, False)
                    for t in range(NT):
                        dve.wait_ge(y_done, E * NT + t + 1 + 3 * NT)
                        dve.wait_ge(y_read, (E - 1) * NT + t + 1 + RING)
                        dve.tensor_tensor(x2[:, t, :], p_y[:, t % RING, :], x2[:, t, :], ALU.add).then_inc(y_read, 1)

                @block.tensor
                def _(pe):
                    for t in range(NT):
                        mm = pe.transpose(p_g[:, t * E:(t + 1) * E], g_rows[:, t * P:(t + 1) * P], id_sb[0:E, 0:E])
                    mm.then_inc(gt_s, 1)

                    def expert(e, b):
                        pe.wait_ge(ewlo_s, e + 3)
                        for t in range(NT):
                            pe.wait_ge(y_read, e * NT + t + 1)
                            for f in range(KF):
                                hi, lo = x2t_hi[:, f, t * P:(t + 1) * P], x2t_lo[:, f, t * P:(t + 1) * P]
                                pe.matmul(p_y[:, t % RING, :], hi, ew_hi[:, b, f, :], start=(f == 0), stop=False)
                                pe.matmul(p_y[:, t % RING, :], hi, ew_lo[:, b, f, :], start=False, stop=False)
                                mm = pe.matmul(p_y[:, t % RING, :], lo, ew_hi[:, b, f, :], start=False, stop=(f == KF - 1))
                            mm.then_inc(y_done, 1)

                    expert(0, 0)
                    pe.wait_ge(sc_step, 18)
                    for t in range(NT):
                        if t == 3 * TC:
                            pe.wait_ge(ct_out, 1)
                        mm = pe.transpose(p_c[:, t // TC % 3, t % TC * P:(t % TC + 1) * P], pr[:, t, :], id_sb[:])
                        if t % TC == TC - 1:
                            mm.then_inc(ct_done, 1)
                    expert(1, 1)
                    with pe.Fori(1, E // 2) as ee:
                        for b in range(2):
                            expert(ee * 2 + b, b)
                    pe.wait_ge(ct_out, NC)
                    for t in range(NT):
                        pe.wait_ge(y_read, E * NT + t + 1)
                        pe.matmul(p_y[:, t % RING, :], comb_t[:, t * P:(t + 1) * P], eb_sb[:], start=True, stop=True).then_inc(y_done, 1)
        late.close()
    return nc


def kernel(x, adj, L0_gnn_W, L0_gnn_a1, L0_gnn_a2, L0_gnn_W1, L0_gnn_b1, L0_gnn_W2, L0_gnn_b2, L0_gnn_W3, L0_gnn_b3,
           L0_gnn_W4, L0_gnn_b4, L0_ffn_gate_W, L0_ffn_gate_b, L0_ffn_expert_W, L0_ffn_expert_b):
    import numpy as np
    from concourse import bacc
    from concourse.bass_utils import run_bass_kernel_spmd

    head_pick = np.zeros((96, H + 1, P), np.float32)
    for k in range(3):
        for h in range(H + 1):
            head_pick[32 * k + h, h] = 1.0
    arrays = {
        "x": np.asarray(x),
        "adj_t": np.asarray(adj).T,
        "w": np.asarray(L0_gnn_W).transpose(1, 0, 2).reshape(F, H * D),
        "a1": np.asarray(L0_gnn_a1).reshape(-1), "a2": np.asarray(L0_gnn_a2).reshape(-1),
        "w1": np.asarray(L0_gnn_W1).T, "b1": np.asarray(L0_gnn_b1).reshape(-1, P).T,
        "w2": np.asarray(L0_gnn_W2).T, "b2": np.asarray(L0_gnn_b2).reshape(-1, P).T,
        "w3": np.asarray(L0_gnn_W3).T, "b3": np.asarray(L0_gnn_b3).reshape(-1, P).T,
        "w4": np.asarray(L0_gnn_W4).T, "b4": np.asarray(L0_gnn_b4),
        "gate_w": np.asarray(L0_ffn_gate_W), "gate_b": np.asarray(L0_ffn_gate_b),
        "expert_w": np.asarray(L0_ffn_expert_W), "expert_b": np.asarray(L0_ffn_expert_b),
        "ident": np.eye(P, dtype=np.float32),
        "head_pick": head_pick.reshape(96, (H + 1) * P),
        "before": np.tril(np.ones((E, E), np.float32), -1).reshape(-1),
    }
    nc = bacc.Bacc("TRN2", target_bir_lowering=False, num_devices=1)
    feeds, aps = {}, []
    for name, a in arrays.items():
        a = np.ascontiguousarray(a)
        feeds["in_" + name] = a
        aps.append(nc.dram_tensor("in_" + name, a.shape, mybir.dt.from_np(a.dtype), kind="ExternalInput").ap())
    aps.append(nc.dram_tensor("out_x", (N, F), F32, kind="ExternalOutput").ap())
    layer_kernel(nc, *aps)
    r = run_bass_kernel_spmd(nc, [feeds], core_ids=[0])
    return r.results[0]["out_x"]
```

```python
from contextlib import ExitStack

import concourse.bass as bass
from concourse import mybir

ALU = mybir.AluOpType
ACT = mybir.ActivationFunctionType
AX = mybir.AxisListType
F32 = mybir.dt.float32
F32R = mybir.dt.float32r
BF16 = mybir.dt.bfloat16
RMAX = bass.bass_isa.ReduceOp.max

P = 128
N = 2048
F = 512
H = 8
D = 64
DX = D + 1
NT = N // P
KF = F // P
CH = 512
NC = N // CH
TC = CH // P
E = 8
PARTS = 3
JG = 4
NG = NT // JG
F1, F2, F3 = 256, 128, 256
ALPHA = 0.2
LN_EPS = 1e-5
GATE_EPS = 1e-4
W_THRES = 0.1
TOPK = 2
NS = (TOPK * N + E * (P - 1)) // P
XR = 3
STEEP = float(2 ** 64)


def layer_kernel(nc, x, adj_t, w, a1, a2, w1, b1, w2, b2, w3, b3, w4, b4,
                 gate_w, gate_b, expert_w, expert_b, ident, head_pick, before, route, prefix, out):
    with ExitStack() as whole:
        def sb(stack, name, shape, dt=F32, side=None):
            return stack.enter_context(nc.sbuf_tensor(name, shape, dt, side=side))

        def ps(stack, name, shape, dt=F32):
            return stack.enter_context(nc.psum_tensor(name, shape, dt))

        def sem(name):
            return whole.enter_context(nc.semaphore(name))

        id_sb = sb(whole, "id_sb", [P, P])
        x_tiles = x.rearrange("(t p) f -> p t f", p=P)
        out_tiles = out.rearrange("(t p) f -> p t f", p=P)
        xn2_d = nc.dram_tensor("xn2_d", (N, F), F32).ap()
        y_d = nc.dram_tensor("y_d", (NS * P, F), F32).ap()
        adj_tiles = adj_t.rearrange("(t p) i -> p t i", p=P)

        sums_kept = ExitStack()
        num = sb(sums_kept, "num", [P, NT, H, DX], side="right")
        colsum = sb(sums_kept, "colsum", [P, H, DX], side="right")

        attention = ExitStack()
        scale = sb(attention, "scale", [P, NT, H, 2])
        adj_bf = sb(attention, "adj_bf", [P, 2, NT, CH], BF16)
        steep_d = sb(attention, "steep_d", [P, NT, H])
        s_rows3 = sb(attention, "s_rows3", [96, N], BF16)
        pick = sb(attention, "pick", [96, H + 1, P], BF16)
        adj_in = sb(attention, "adj_in", [P, 2, CH])

        prep = ExitStack()
        sd = sb(prep, "sd", [P, NT, 2 * H], side="right")
        dmax = sb(prep, "dmax", [P, H], side="right")
        dtop = sb(prep, "dtop", [P, H], side="right")
        ex = sb(prep, "ex", [P, 2, NT, H], side="right")
        q = sb(prep, "q", [P, NT, H], side="right")
        m = sb(prep, "m", [P, NT, H], side="right")
        arg = sb(prep, "arg", [P, NT, H, 2], side="right")

        rows = adj_bf[0:2 * H, 1].rearrange("p t i -> p (t i)").bitcast(F32)[:, 0:N]
        with ExitStack() as st:
            xs = sb(st, "xs", [P, NT, F])
            xt_hi = sb(st, "xt_hi", [P, 2, KF, CH], F32R)
            xt_lo = sb(st, "xt_lo", [P, 2, KF, CH], F32R)
            xn = sb(st, "xn", [P, TC, F])
            adj_in2 = sb(st, "adj_in2", [P, 2, CH])
            w_raw = sb(st, "w_raw", [P, KF, F])
            w_hi = sb(st, "w_hi", [P, KF, F], F32R)
            w_lo = sb(st, "w_lo", [P, KF, F], F32R)
            a_in = sb(st, "a_in", [P, 2, F])
            wa_prod = sb(st, "wa_prod", [P, 2, KF, F])
            wa = sb(st, "wa", [P, KF, 2 * H])
            wa_hi = sb(st, "wa_hi", [P, KF, 2 * H], F32R)
            wa_lo = sb(st, "wa_lo", [P, KF, 2 * H], F32R)
            stats = sb(st, "stats", [P, NT, 6])
            mv = sb(st, "mv", [P, NT, 2])
            rstd = sb(st, "rstd", [P, NT])
            half = sb(st, "half", [P, TC])
            eps = sb(st, "eps", [P, TC])
            rest = sb(st, "rest", [H, CH])
            part2 = sb(st, "part2", [H, CH], BF16)
            p_x = ps(st, "p_x", [P, KF, CH])
            p_wh = ps(st, "p_wh", [P, 2, F])
            p_rows = ps(st, "p_rows", [2 * H, CH])
            p_sd = ps(st, "p_sd", [P, NT, 2 * H])

            id_in, w_in, a_in_s = sem("id_in"), sem("w_in"), sem("a_in_s")
            x_in = [sem(f"x_in{k}") for k in range(NC)]
            x0_in = [sem(f"x0_in{u}") for u in range(TC)]
            stat_done, zero_s, p1_s, rest_s, p2_s = sem("stat_done"), sem("zero_s"), sem("p1_s"), sem("rest_s"), sem("p2_s")
            a0_in, a0_read = [sem("a0_in0"), sem("a0_in1")], sem("a0_read")
            whi_done, wlo_done, wa_step, wa_cut = sem("whi_done"), sem("wlo_done"), sem("wa_step"), sem("wa_cut")
            wa_sum, pick_s = sem("wa_sum"), sem("pick_s")
            half_done, var_done, mean_done, rstd_done, xn_done = (
                sem("half_done"), sem("var_done"), sem("mean_done"), sem("rstd_done"), sem("xn_done"))
            xt_done, xhi_done, xlo_done = sem("xt_done"), sem("xhi_done"), sem("xlo_done")
            wh_done, wh_out, rows_done, rows_out = sem("wh_done"), sem("wh_out"), sem("rows_done"), sem("rows_out")
            ones_done = sem("ones_done")
            sd_done, sd_out, dmax_done, dtop_done = sem("sd_done"), sem("sd_out"), sem("dmax_done"), sem("dtop_done")
            arg_done, m_step, ex_done, scale_done = sem("arg_done"), sem("m_step"), sem("ex_done"), sem("scale_done")

            with nc.Block() as block:
                @block.sync
                def _(sp):
                    def load(k):
                        sp.dma_start(xs[:, k * TC:(k + 1) * TC, :], x_tiles[:, k * TC:(k + 1) * TC, :]).then_inc(x_in[k], 16)

                    for u in range(TC):
                        sp.dma_start(xs[:, u, :], x_tiles[:, u, :]).then_inc(x0_in[u], 16)
                    sp.dma_start(w_raw[:], w.rearrange("(k p) c -> p k c", p=P)).then_inc(w_in, 16)
                    sp.dma_start(id_sb[:], ident).then_inc(id_in, 16)
                    sp.dma_start(a_in[:, 0, :], a1.partition_broadcast(P)).then_inc(a_in_s, 16)
                    sp.dma_start(a_in[:, 1, :], a2.partition_broadcast(P)).then_inc(a_in_s, 16)
                    for k in range(1, NC):
                        load(k)
                    sp.dma_start(pick[:].rearrange("p h c -> p (h c)"), head_pick).then_inc(pick_s, 16)
                    for j in range(NT // 2):
                        if j >= 2:
                            sp.wait_ge(a0_read, j - 1)
                        sp.dma_start((adj_in, adj_in2)[j % 2][:], adj_tiles[:, j * 2:(j + 1) * 2, 0:CH]).then_inc(a0_in[j % 2], 16)

                @block.gpsimd
                def _(pool):
                    pool.memset(half[:], -0.5).then_inc(half_done, 1)
                    pool.memset(eps[:], LN_EPS).then_inc(half_done, 1)
                    pool.memset(num[:, :, :, D:DX], 1.0).then_inc(ones_done, 1)
                    pool.memset(colsum[:, :, D:DX], float(N)).then_inc(ones_done, 1)
                    pool.wait_ge(half_done, 2)

                    def deviation(k):
                        mine = rstd[:, k * TC:(k + 1) * TC]
                        pool.wait_ge(mean_done, TC * (k + 1))
                        pool.tensor_tensor(mine, mv[:, k * TC:(k + 1) * TC, 1], eps[:], ALU.add).then_inc(var_done, 1)
                        pool.wait_ge(var_done, k + 1)
                        pool.tensor_tensor(mine, mine, half[:], ALU.pow).then_inc(rstd_done, 1)

                    deviation(0)
                    pool.wait_ge(w_in, 16)
                    pool.wait_ge(a_in_s, 32)
                    for i in range(2):
                        pool.tensor_tensor(wa_prod[:, i], w_raw[:], a_in[:, i:i + 1, :].broadcast_to([P, KF, F]), ALU.mult).then_inc(wa_step, 1)
                        if i == 0:
                            deviation(1)
                    for k in range(2, NC):
                        deviation(k)
                    for j in range(NT // 2):
                        pool.wait_ge(a0_in[j % 2], 16 * (j // 2 + 1))
                        pool.tensor_scalar(adj_bf[:, 0, j * 2:(j + 1) * 2, :], (adj_in, adj_in2)[j % 2][:], 0.0, None, ALU.is_gt).then_inc(a0_read, 1)
                    pool.wait_ge(dmax_done, 1)
                    pool.partition_all_reduce(dtop[:], dmax[:], P, RMAX).then_inc(dtop_done, 1)

                @block.vector
                def _(dve):
                    def statistics(k):
                        if k:
                            dve.wait_ge(x_in[k], 16)
                        tiles = range(k * TC, (k + 1) * TC)
                        for t in tiles:
                            if k == 0:
                                dve.wait_ge(x0_in[t], 16)
                            dve.bn_stats(stats[:, t, :], xs[:, t, :]).then_inc(stat_done, 1)
                        for t in tiles:
                            dve.wait_ge(stat_done, t + 1)
                            dve.bn_aggr(mv[:, t, :], stats[:, t, :]).then_inc(mean_done, 1)

                    def normalise(k):
                        dve.wait_ge(rstd_done, k + 1)
                        if k:
                            dve.wait_ge(xt_done, k * KF)
                        for u in range(TC):
                            t = k * TC + u
                            dve.tensor_scalar(xn[:, u, :], xs[:, t, :], mv[:, t, 0:1], rstd[:, t:t + 1], ALU.subtract, ALU.mult).then_inc(xn_done, 1)

                    def cut_lo(k):
                        for f in range(KF):
                            dve.wait_ge(xhi_done, k * KF + f + 1)
                            dve.tensor_tensor(xt_lo[:, k % 2, f, :], p_x[:, f, :], xt_hi[:, k % 2, f, :].bitcast(F32),
                                              ALU.subtract).then_inc(xlo_done, 1)

                    def logit_weight(i):
                        dve.wait_ge(wa_step, i + 1)
                        dve.tensor_reduce(wa[:, :, i * H:(i + 1) * H], wa_prod[:, i].rearrange("p k (h d) -> p k h d", h=H),
                                          AX.X, ALU.add).then_inc(wa_sum, 1)

                    def cut_rows(k):
                        here = slice(k * CH, (k + 1) * CH)
                        dve.wait_ge(p1_s, k + 1)
                        if k:
                            dve.wait_ge(rest_s, 4 * k)
                        dve.tensor_tensor(rest[:], rows[0:H, here], s_rows3[0:H, here], ALU.subtract).then_inc(rest_s, 1)
                        dve.wait_ge(rest_s, 4 * k + 1)
                        if k:
                            dve.wait_ge(p2_s, k)
                        dve.tensor_copy(part2[:], rest[:]).then_inc(rest_s, 1)
                        dve.wait_ge(rest_s, 4 * k + 2)
                        dve.tensor_tensor(rest[:], rest[:], part2[:], ALU.subtract).then_inc(rest_s, 1)
                        dve.wait_ge(rest_s, 4 * k + 3)
                        dve.tensor_copy(s_rows3[64:64 + H, here], rest[:]).then_inc(rest_s, 1)

                    dve.memzero(s_rows3[:].bitcast(mybir.dt.uint32)).then_inc(zero_s, 1)
                    statistics(0)
                    normalise(0)
                    dve.wait_ge(whi_done, 1)
                    dve.tensor_tensor(w_lo[:], w_raw[:], w_hi[:].bitcast(F32), ALU.subtract).then_inc(wlo_done, 1)
                    cut_lo(0)
                    statistics(1)
                    logit_weight(0)
                    normalise(1)
                    logit_weight(1)
                    dve.wait_ge(wa_sum, 2)
                    dve.tensor_copy(wa_hi[:], wa[:]).then_inc(wa_cut, 1)
                    dve.wait_ge(wa_cut, 1)
                    dve.tensor_tensor(wa_lo[:], wa[:], wa_hi[:].bitcast(F32), ALU.subtract).then_inc(wa_cut, 1)
                    statistics(2)
                    for k in range(1, NC):
                        cut_lo(k)
                        if k + 1 < NC:
                            normalise(k + 1)
                        if k + 2 < NC:
                            statistics(k + 2)
                        if k == 1:
                            cut_rows(0)
                        cut_rows(k)
                    dve.wait_ge(sd_done, 1)
                    dve.tensor_copy(sd[:], p_sd[:]).then_inc(sd_out, 1)
                    dve.wait_ge(sd_out, 1)
                    dve.tensor_reduce(dmax[:], sd[:, :, H:2 * H].rearrange("p t h -> p h t"), AX.X, ALU.max).then_inc(dmax_done, 1)
                    dve.tensor_scalar(steep_d[:], sd[:, :, H:2 * H], STEEP, None, ALU.mult).then_inc(m_step, 1)
                    dve.wait_ge(dtop_done, 1)
                    top = dtop[:].rearrange("p (a h) -> p a h", a=1).broadcast_to([P, NT, H])
                    dve.tensor_tensor(ex[:, 0], sd[:, :, H:2 * H], top, ALU.subtract).then_inc(arg_done, 1)
                    dve.tensor_tensor(q[:], sd[:, :, 0:H], top, ALU.add).then_inc(m_step, 1)
                    dve.wait_ge(m_step, 2)
                    dve.scalar_tensor_tensor(m[:], q[:], ALPHA, q[:], ALU.mult, ALU.max).then_inc(m_step, 1)
                    dve.wait_ge(m_step, 3)
                    dve.tensor_tensor(arg[:, :, :, 0], q[:], m[:], ALU.subtract).then_inc(m_step, 1)
                    dve.scalar_tensor_tensor(arg[:, :, :, 1], q[:], ALPHA, m[:], ALU.mult, ALU.subtract).then_inc(m_step, 1)

                @block.scalar
                def _(act):
                    act.wait_ge(w_in, 16)
                    act.activation(w_hi[:], w_raw[:], ACT.Copy).then_inc(whi_done, 1)

                    def cut_hi(k):
                        for f in range(KF):
                            act.wait_ge(xt_done, k * KF + f + 1)
                            act.activation(xt_hi[:, k % 2, f, :], p_x[:, f, :], ACT.Copy).then_inc(xhi_done, 1)

                    def wh_copy(k, tiles):
                        for u in tiles:
                            t = k * TC + u
                            act.wait_ge(wh_done, t + 1)
                            act.activation(num[:, t, :, 0:D], p_wh[:, u % 2, :].rearrange("p (h d) -> p h d", h=H), ACT.Copy).then_inc(wh_out, 1)

                    def rows_copy(k):
                        here = slice(k * CH, (k + 1) * CH)
                        act.wait_ge(rows_done, k + 1)
                        act.activation(rows[:, here], p_rows[:], ACT.Copy).then_inc(rows_out, 1)
                        act.wait_ge(rows_out, k + 1)
                        act.activation(s_rows3[0:H, here], rows[0:H, here], ACT.Copy).then_inc(p1_s, 1)

                    def second_part(k):
                        act.wait_ge(rest_s, 4 * k + 2)
                        act.activation(s_rows3[32:32 + H, k * CH:(k + 1) * CH], part2[:], ACT.Copy).then_inc(p2_s, 1)

                    def exponentials():
                        act.wait_ge(arg_done, 1)
                        act.activation(ex[:, 1], ex[:, 0], ACT.Exp, scale=ALPHA).then_inc(ex_done, 1)
                        act.wait_ge(ex_done, 1)
                        act.activation(ex[:, 0], ex[:, 0], ACT.Exp).then_inc(ex_done, 1)
                        act.wait_ge(m_step, 5)
                        act.activation(scale[:], arg[:], ACT.Exp).then_inc(scale_done, 1)

                    cut_hi(0)
                    act.wait_ge(zero_s, 1)
                    for k in range(NC):
                        if k:
                            second_part(k - 1)
                            rows_copy(k)
                        wh_copy(k, (0, 1))
                        if k + 1 < NC:
                            cut_hi(k + 1)
                        if k == NC - 1:
                            second_part(k)
                            exponentials()
                        wh_copy(k, (2, 3))
                        if k == 0:
                            rows_copy(k)
                        if k == 1:
                            act.wait_ge(pick_s, 16)
                @block.tensor
                def _(pe):
                    pe.wait_ge(id_in, 16)

                    def turn(k):
                        for u in range(TC):
                            pe.wait_ge(xn_done, k * TC + u + 1)
                            for f in range(KF):
                                mm = pe.transpose(p_x[:, f, u * P:(u + 1) * P],
                                                  xn[:, u, f * P:(f + 1) * P], id_sb[:])
                                if u == TC - 1:
                                    mm.then_inc(xt_done, 1)

                    def wh(k, tiles):
                        for u in tiles:
                            if k * TC + u >= 2:
                                pe.wait_ge(wh_out, k * TC + u - 1)
                            for f in range(KF):
                                hi, lo = (t[:, k % 2, f, u * P:(u + 1) * P] for t in (xt_hi, xt_lo))
                                pe.matmul(p_wh[:, u % 2, :], hi, w_hi[:, f, :], start=(f == 0), stop=False)
                                pe.matmul(p_wh[:, u % 2, :], hi, w_lo[:, f, :], start=False, stop=False)
                                mm = pe.matmul(p_wh[:, u % 2, :], lo, w_hi[:, f, :], start=False, stop=(f == KF - 1))
                            mm.then_inc(wh_done, 1)

                    def logits(k):
                        if k:
                            pe.wait_ge(rows_out, k)
                        for n, (l, r) in enumerate([(wa_hi, xt_hi), (wa_hi, xt_lo), (wa_lo, xt_hi)]):
                            for f in range(KF):
                                mm = pe.matmul(p_rows[:], l[:, f, :], r[:, k % 2, f, :], start=(n + f == 0), stop=(n == 2 and f == KF - 1))
                        mm.then_inc(rows_done, 1)

                    turn(0)
                    pe.wait_ge(wlo_done, 1)
                    for k in range(NC):
                        pe.wait_ge(xlo_done, (k + 1) * KF)
                        if k:
                            logits(k)
                        wh(k, (0, 1))
                        if k + 1 < NC:
                            turn(k + 1)
                        else:
                            pe.wait_ge(rows_out, NC)
                            for t in range(NT):
                                mm = pe.transpose(p_sd[:, t, :], rows[:, t * P:(t + 1) * P], id_sb[0:2 * H, 0:2 * H])
                            mm.then_inc(sd_done, 1)
                        wh(k, (2, 3))
                        if k == 0:
                            pe.wait_ge(wa_cut, 2)
                            logits(k)

        uv = sb(attention, "uv", [P, NT, H, 2, PARTS, DX], BF16)
        with ExitStack() as st:
            ones = sb(st, "ones", [P, P])
            wgt = sb(st, "wgt", [P, 2, 2, 2, H, DX])
            p_cs = ps(st, "p_cs", [P, F])
            shift_s = sem("shift_s")
            ones_s, cs_done, cs_out = sem("ones_s"), sem("cs_done"), sem("cs_out")
            wgt_done, cut1, rest1, cut2, cut3 = sem("wgt_done"), sem("cut1"), sem("rest1"), sem("cut2"), sem("cut3")
            def part(t, s, i):
                return uv[:, bass.ds(t, 1), :, s, i, :].rearrange("p a h d -> p (a h) d")

            def skewed(eng, ahead_of, behind):
                ahead_of(0, 0)
                with eng.Fori(0, NT // 2 - 1) as tt:
                    for b in range(2):
                        ahead_of(tt * 2 + b + 1, 1 - b)
                        behind(tt * 2 + b, b)
                ahead_of(NT - 1, 1)
                behind(NT - 2, 0)
                behind(NT - 1, 1)

            with nc.Block() as block:
                @block.sync
                def _(sp):
                    for q in range(0, 96, 32):
                        sp.dma_start(s_rows3[q + H:q + H + 1, 0:N - CH], s_rows3[q:q + 1, CH:N]).then_inc(shift_s, 16)
                    sp.wait_ge(shift_s, 48)

                @block.tensor
                def _(pe):
                    pe.wait_ge(ones_s, 1)
                    for t in range(NT):
                        mm = pe.matmul(p_cs[:], ones[:], num[:, t, :, 0:D], start=(t == 0), stop=(t == NT - 1))
                    mm.then_inc(cs_done, 1)

                @block.vector
                def _(dve):
                    dve.memset(ones[:], 1.0).then_inc(ones_s, 1)
                    dve.sem_inc(rest1, 4)
                    dve.sem_inc(cut3, 4)

                    def rest_of(t, b):
                        for s in range(2):
                            dve.wait_ge(cut1, 2 * t + s + 1)
                            dve.wait_ge(cut3, 2 * t + s + 1)
                            dve.tensor_tensor(wgt[:, b, 1, s], wgt[:, b, 0, s], part(t, s, 0), ALU.subtract).then_inc(rest1, 1)

                    def third_of(t, b):
                        for s in range(2):
                            dve.wait_ge(cut2, 2 * t + s + 1)
                            dve.tensor_tensor(part(t, s, 2), wgt[:, b, 1, s], part(t, s, 1), ALU.subtract).then_inc(cut3, 1)

                    skewed(dve, rest_of, third_of)

                @block.gpsimd
                def _(pool):
                    with pool.Fori(0, NT // 2) as tt:
                        for b in range(2):
                            for s in range(2):
                                t = tt * 2 + b
                                pool.wait_ge(rest1, 2 * t + s + 1)
                                pool.tensor_tensor(wgt[:, b, 0, s], num[:, bass.ds(t, 1), :, :].rearrange("p a h d -> p (a h) d"),
                                                   ex[:, s, bass.ds(t, 1), :].rearrange("p a h -> p (a h)").unsqueeze(2).broadcast_to([P, H, DX]),
                                                   ALU.mult).then_inc(wgt_done, 1)

                @block.scalar
                def _(act):

                    def first_of(t, b):
                        for s in range(2):
                            act.wait_ge(wgt_done, 2 * t + s + 1)
                            act.activation(part(t, s, 0), wgt[:, b, 0, s], ACT.Copy).then_inc(cut1, 1)

                    def second_of(t, b):
                        for s in range(2):
                            act.wait_ge(rest1, 2 * t + s + 5)
                            act.activation(part(t, s, 1), wgt[:, b, 1, s], ACT.Copy).then_inc(cut2, 1)

                    skewed(act, first_of, second_of)
                    act.wait_ge(cs_done, 1)
                    act.activation(colsum[:, :, 0:D], p_cs[:].rearrange("p (h d) -> p h d", h=H), ACT.Copy).then_inc(cs_out, 1)

        prep.close()

        RB = 2
        HT = NG * TC
        with ExitStack() as st:
            m1 = sb(st, "m1", [P, NG, JG, CH], BF16)
            m0 = sb(st, "m0", [P, RB, JG, CH], BF16)
            sums = sb(st, "sums", [P, 2, TC, 2, DX])
            parts = sb(st, "parts", [P, TC // 2, 2, PARTS, DX])
            fill = sb(st, "fill", [P, P], BF16)
            empty = sb(st, "empty", [P, TC])
            p_acc = ps(st, "p_acc", [P, TC, CH])
            p_s = ps(st, "p_s", [P, 2, CH])
            adj_in_s, conv_done = sem("adj_in_s"), sem("conv_done")
            s_ready, relu_done, m1_ready, m1_used, m0_ready = (
                sem("s_ready"), sem("relu_done"), sem("m1_ready"), sem("m1_used"), sem("m0_ready"))
            tiles_done, acc_read, sums_used, scaled, fill_s = (
                sem("tiles_done"), sem("acc_read"), sem("sums_used"), sem("scaled"), sem("fill_s"))
            acc_copied, parts_used = sem("acc_copied"), sem("parts_used")
            DXX = 2 * PARTS * DX
            HALF = TC // 2

            def scale_head(eng, n, c, h, hb):
                half = sums[:, hb, 0:HALF]
                eng.wait_ge(sums_used, n + 2)
                eng.wait_ge(acc_copied, HALF * n + 2 * HALF)
                eng.tensor_tensor(half, parts[:, :, :, 0, :], parts[:, :, :, 1, :], ALU.add).then_inc(scaled, 1)
                eng.wait_ge(scaled, 5 * n + 1)
                eng.tensor_tensor(half, half, parts[:, :, :, 2, :], ALU.add).then_inc(parts_used, 1)
                eng.wait_ge(parts_used, n + 3)
                eng.wait_ge(acc_read, HALF * n + 2 * HALF)
                eng.tensor_tensor(sums[:, hb], sums[:, hb],
                                   scale[:, c * TC:(c + 1) * TC, h, :].unsqueeze(3).broadcast_to([P, TC, 2, DX]),
                                   ALU.mult).then_inc(scaled, 1)
                mine = num[:, c * TC:(c + 1) * TC, h, :]
                eng.wait_ge(scaled, 5 * n + 2)
                eng.tensor_tensor(mine, sums[:, hb, :, 0, :], sums[:, hb, :, 1, :], ALU.add).then_inc(scaled, 1)
                eng.wait_ge(scaled, 5 * n + 3)
                eng.tensor_scalar(empty[:], num[:, c * TC:(c + 1) * TC, h, D], 0.0, None, ALU.is_equal).then_inc(scaled, 1)
                eng.wait_ge(scaled, 5 * n + 4)
                mean = sums[:, hb, :, 0, :]
                eng.tensor_tensor(mean, colsum[:, h:h + 1, :].broadcast_to([P, TC, DX]),
                                   empty[:].unsqueeze(2).broadcast_to([P, TC, DX]), ALU.mult).then_inc(scaled, 1)
                eng.wait_ge(scaled, 5 * n + 5)
                eng.tensor_tensor(mine, mine, mean, ALU.add).then_inc(sums_used, 1)

            def heads(eng, body):
                with eng.Fori(0, NC // 2) as cc:
                    for cb in range(2):
                        with eng.Fori(0, H // 2) as hh:
                            for hb in range(2):
                                body((cc * 2 + cb) * H + hh * 2 + hb, cc * 2 + cb, hh * 2 + hb, hb, cb)

            with nc.Block() as block:
                @block.sync
                def _(sp):
                    for c in range(1, NC):
                        with sp.Fori(0, NT // 2) as j:
                            sp.wait_ge(conv_done, (c - 1) * (NT // 2) + 1 + j)
                            sp.dma_start(adj_in[:], adj_tiles[:, bass.ds(j * 2, 2), c * CH:(c + 1) * CH]).then_inc(adj_in_s, 16)

                @block.gpsimd
                def _(pool):
                    pool.sem_inc(conv_done, 1)
                    pool.sem_inc(sums_used, 3)
                    pool.sem_inc(parts_used, 2)

                    for c in range(NC):
                        if c >= 1 and c < NC - 1:
                            pool.wait_ge(m0_ready, c * H * NG + NG)
                        for h in range(H):
                            if c < NC - 1:
                                pool.wait_ge(adj_in_s, (c * H + 1 + h) * 16)
                                pool.tensor_scalar(adj_bf[:, (c + 1) % 2, h * 2:(h + 1) * 2, :], adj_in[:], 0.0, None,
                                                   ALU.is_gt).then_inc(conv_done, 1)
                            if c * H + h < NC * H - 1:
                                scale_head(pool, c * H + h, c, h, h % 2)

                @block.scalar
                def _(act):
                    act.sem_inc(relu_done, 2 * NG * JG)

                    def evacuate(n):
                        act.wait_ge(parts_used, n + 1)
                        for i in range(HALF):
                            act.wait_ge(tiles_done, n * HT + TC + i + 1)
                            act.activation(parts[:, i].rearrange("p m k d -> p (m k d)"), p_acc[:, i, 0:DXX], ACT.Copy).then_inc(acc_copied, 1)

                    def body(n, c, h, hb, cb):
                        act.wait_ge(s_ready, n + 1)
                        for g in range(NG):
                            if g == NG - 2:
                                evacuate(n)
                            act.wait_ge(m1_used, n * NG + g + 1)
                            act.wait_ge(m0_ready, n * NG + g + 1)
                            for j in range(JG):
                                t = g * JG + j
                                act.activation(m1[:, g, j, :], p_s[:, hb, :], ACT.Relu, scale=STEEP,
                                               bias=steep_d[:, t, bass.ds(h, 1)]).then_inc(relu_done, 1)

                    heads(act, body)
                    evacuate(NC * H)

                @block.vector
                def _(dve):
                    dve.sem_inc(m0_ready, NG)
                    dve.memset(fill[:], 0.0).then_inc(fill_s, 1)

                    def evacuate(n, hb):
                        dve.wait_ge(sums_used, n + 1)
                        for i in range(HALF, TC):
                            dve.wait_ge(tiles_done, n * HT + TC + i + 1)
                            dve.tensor_reduce(sums[:, 1 - hb, i], p_acc[:, i, 0:DXX].rearrange("p (m k d) -> p m d k", m=2, k=PARTS),
                                              AX.X, ALU.add).then_inc(acc_read, 1)

                    def body(n, c, h, hb, cb):
                        dve.wait_ge(conv_done, c * (NT // 2) + 1)
                        for g in range(NG):
                            edges = adj_bf[:, cb, g * JG:(g + 1) * JG, :]
                            dve.wait_ge(relu_done, (n * NG + g) * JG + (2 * NG + 1) * JG)
                            dve.tensor_tensor(m1[:, g], m1[:, g], edges, ALU.min).then_inc(m1_ready, 1)
                            dve.wait_ge(tiles_done, (n * NG + g) * TC + TC)
                            dve.wait_ge(m1_ready, n * NG + g + 1)
                            dve.tensor_tensor(m0[:, g % RB], edges, m1[:, g], ALU.subtract).then_inc(m0_ready, 1)
                            if g == 0:
                                evacuate(n, hb)

                    heads(dve, body)
                    evacuate(NC * H, 0)
                    dve.wait_ge(sums_used, NC * H + 2)
                    scale_head(dve, NC * H - 1, NC - 1, H - 1, (H - 1) % 2)

                @block.tensor
                def _(pe):
                    pe.sem_inc(m1_used, NG)
                    pe.sem_inc(tiles_done, TC)
                    pe.matmul(p_s[:, 0, :], pick[:, 0, :], s_rows3[:, 0:CH], start=True, stop=True).then_inc(s_ready, 1)
                    pe.wait_ge(fill_s, 1)
                    for i in range(TC):
                        pe.matmul(p_acc[:, i, :], fill[:], fill[:, 0:1].broadcast_to([P, CH]), start=True, stop=True).then_inc(tiles_done, 1)

                    def body(n, c, h, hb, cb):
                        for g in range(NG):
                            if g == 1:
                                pe.wait_ge(relu_done, n * NG * JG + 2 * NG * JG)
                                pe.matmul(p_s[:, 1 - hb, :], pick[:, bass.ds(h + 1, 1), :].rearrange("p a c -> p (a c)"),
                                          s_rows3[:, bass.ds(c * CH, CH)], start=True, stop=True).then_inc(s_ready, 1)
                            pe.wait_ge(m1_ready, n * NG + g + 1)
                            for i in range(TC):
                                if g == 0:
                                    if i < HALF:
                                        pe.wait_ge(acc_copied, n * HALF + i + 1)
                                    else:
                                        pe.wait_ge(acc_read, n * HALF + i - HALF + 1)
                                for j in range(JG):
                                    mm = pe.matmul(p_acc[:, i, 0:DXX // 2], m1[:, g, j, i * P:(i + 1) * P],
                                                   uv[:, g * JG + j, bass.ds(h, 1), 0].rearrange("p a k d -> p (a k d)"),
                                                   start=(g == 0 and j == 0), stop=False, skip_group_check=True)
                            mm.then_inc(m1_used, 1)
                            pe.wait_ge(m0_ready, n * NG + g + 1 + NG)
                            for i in range(TC):
                                for j in range(JG):
                                    mm = pe.matmul(p_acc[:, i, DXX // 2:DXX], m0[:, g % RB, j, i * P:(i + 1) * P],
                                                   uv[:, g * JG + j, bass.ds(h, 1), 1].rearrange("p a k d -> p (a k d)"),
                                                   start=False, stop=(g == NG - 1 and j == JG - 1), skip_group_check=True)
                                mm.then_inc(tiles_done, 1)

                    heads(pe, body)
        attention.close()

        late = ExitStack()
        x2 = sb(late, "x2", [P, NT, F])
        scores = sb(late, "scores", [P, NT, E])
        sel = sb(late, "sel", [P, NT, E])
        prefix_sb = sb(late, "prefix_sb", [P, 2, P], BF16)
        gb_sb = sb(late, "gb_sb", [P, E])
        tri = sb(late, "tri", [P, E * E])
        raw_kept = ExitStack()
        ew_raw = sb(raw_kept, "ew_raw", [P, E, KF, F])
        spare_in = sem("spare_in")
        ew_in, small_in, xn2_out, choice_s = sem("ew_in"), sem("small_in"), sem("xn2_out"), sem("choice_s")
        with ExitStack() as st:
            layers = [("w1", w1, F, F1), ("w2", w2, F1, F2), ("w3", w3, F2, F3), ("w4", w4, F3, F), ("gate", gate_w, F, E)]
            cut = {}
            for name, src, k, m_ in layers:
                cut[name] = (sb(st, name + "_hi", [P, k // P, m_], F32R), sb(st, name + "_lo", [P, k // P, m_], F32R))
            b1_sb, b2_sb, b3_sb = sb(st, "b1_sb", [P, F1 // P]), sb(st, "b2_sb", [P, F2 // P]), sb(st, "b3_sb", [P, F3 // P])
            b4_sb = sb(st, "b4_sb", [P, F])
            h_sb = sb(st, "h_sb", [P, 2, TC, F])
            e_sb = sb(st, "e_sb", [P, TC, F])
            et_hi = sb(st, "et_hi", [P, KF, CH], F32R)
            et_lo = sb(st, "et_lo", [P, KF, CH], F32R)
            y_f = sb(st, "y_f", [P, 2, CH])
            g_rows = y_f[0:E, 0, :]
            y_hi = sb(st, "y_hi", [P, 2, CH], F32R)
            y_lo = sb(st, "y_lo", [P, 2, CH], F32R)
            rden = sb(st, "rden", [P, TC, H])
            stats = sb(st, "stats2", [P, TC, 6])
            mv = sb(st, "mv2", [P, TC, 2])
            rstd = sb(st, "rstd2", [P, TC])
            half = sb(st, "half2", [P, TC])
            eps = sb(st, "eps2", [P, TC])
            p_t = ps(st, "p_t", [P, KF, CH])
            p_m = ps(st, "p_m", [P, 4, CH])
            raw_in = [sem(f"raw_in{i}") for i in range(5)]
            b_in, raw_hi, raw_lo = sem("b_in"), sem("raw_hi"), sem("raw_lo")
            xb_in = [sem(f"xb_in{c}") for c in range(NC)]
            half_s, rden_s, h_out, min_s = sem("half_s"), sem("rden_s"), sem("h_out"), sem("min_s")
            exp_s, enc_s, gr_out, g_turned = sem("exp_s"), sem("enc_s"), sem("gr_out"), sem("g_turned")
            turned, e_hi, e_lo = sem("turned"), sem("e_hi"), sem("e_lo")
            mm_done, y_act, y_cut = sem("mm_done"), sem("y_act"), sem("y_cut")
            xb_s, x2_s, stat_s, mean_s, var_s, rstd_s = (
                sem("xb_s"), sem("x2_s"), sem("stat_s"), sem("mean_s"), sem("var_s"), sem("rstd_s"))
            xn2_s, turned2, n_hi, n_lo, g_done, g_out = (
                sem("xn2_s"), sem("turned2"), sem("n_hi"), sem("n_lo"), sem("g_done"), sem("g_out"))

            raw, at = {}, 0
            flat = x2[:].rearrange("p t f -> p (t f)")
            for name, src, k, m_ in layers:
                raw[name] = flat[:, at:at + k // P * m_].rearrange("p (k m) -> p k m", m=m_)
                at += k // P * m_

            def spare(c):
                return num[:, c * TC:(c + 1) * TC].rearrange("p t h d -> p (t h d)")[:, 0:TC * F].rearrange("p (t f) -> p t f", f=F)

            def choose(dve, tiles, gt, eq):
                count = tiles.stop - tiles.start
                mine = scores[:, tiles]
                gt, eq = (a.rearrange("p (t e f) -> p t e f", t=count, e=E) for a in (gt, eq))
                other = mine.unsqueeze(2).broadcast_to([P, count, E, E])
                own = mine.unsqueeze(3).broadcast_to([P, count, E, E])
                tri_e = tri[:].rearrange("p (e f) -> p e f", e=E).unsqueeze(1).broadcast_to([P, count, E, E])
                yield dve.tensor_tensor(mine, mine, gb_sb[:].unsqueeze(1).broadcast_to([P, count, E]), ALU.add)
                yield dve.tensor_scalar(mine, mine, GATE_EPS, None, ALU.max)
                yield dve.tensor_tensor(eq, other, own, ALU.is_equal)
                yield dve.tensor_tensor(eq, eq, tri_e, ALU.mult)
                yield dve.tensor_tensor(gt, other, own, ALU.is_gt)
                yield dve.tensor_tensor(gt, gt, eq, ALU.add)
                yield dve.tensor_reduce(sel[:, tiles], gt, AX.X, ALU.add)
                yield dve.tensor_scalar(sel[:, tiles], sel[:, tiles], float(TOPK), None, ALU.is_lt)

            def steps(stage_parts):
                for k in range(-1, NC + 2):
                    for lag, part in stage_parts:
                        if 0 <= k - lag < NC:
                            part(k - lag)

            def heads_out(eng, c):
                mine = num[:, c * TC:(c + 1) * TC]
                eng.wait_ge(rden_s, c + 1)
                if c >= 2:
                    eng.wait_ge(turned, (c - 1) * KF)
                eng.tensor_tensor(h_sb[:, c % 2].rearrange("p t (h d) -> p t h d", h=H), mine[:, :, :, 0:D],
                                  rden[:].unsqueeze(3).broadcast_to([P, TC, H, D]), ALU.mult).then_inc(h_out, 1)

            with nc.Block() as block:
                @block.sync
                def _(sp):
                    for i, (name, src, k, m_) in enumerate(layers):
                        sp.dma_start(raw[name], src.rearrange("(k p) m -> p k m", p=P)).then_inc(raw_in[i], 16)
                    for dst, src in ((b1_sb, b1), (b2_sb, b2), (b3_sb, b3)):
                        sp.dma_start(dst[:], src).then_inc(b_in, 16)
                    sp.dma_start(b4_sb[:], b4.partition_broadcast(P)).then_inc(b_in, 16)
                    for dst, src in ((gb_sb[:], gate_b.partition_broadcast(P)), (tri[:], before.partition_broadcast(P)),
                                     (prefix_sb[:].rearrange("p a c -> p (a c)"), prefix)):
                        sp.dma_start(dst, src).then_inc(small_in, 16)

                    def load(c):
                        sp.wait_ge(h_out, c + 1)
                        sp.dma_start(spare(c), x_tiles[:, c * TC:(c + 1) * TC, :]).then_inc(xb_in[c], 16)
                        for e in range(c * E // NC, (c + 1) * E // NC):
                            sp.dma_start(ew_raw[:, e], expert_w[e].rearrange("(k p) f -> p k f", p=P)).then_inc(ew_in, 16)

                    def store_norm(c):
                        sp.wait_ge(xn2_s, (c + 1) * TC)
                        sp.dma_start(xn2_d.rearrange("(t p) f -> p t f", p=P)[:, c * TC:(c + 1) * TC, :], spare(c)).then_inc(xn2_out, 16)

                    sp.dma_start(y_d[TOPK * N:, :], x[0:NS * P - TOPK * N, :]).then_inc(spare_in, 16)

                    steps([(0, load), (2, store_norm)])
                    sp.wait_ge(spare_in, 16)

                @block.gpsimd
                def _(pool):
                    pool.memset(half[:], -0.5).then_inc(half_s, 1)
                    pool.memset(eps[:], LN_EPS).then_inc(half_s, 1)
                    pool.wait_ge(half_s, 2)

                    def heads(c):
                        if c:
                            heads_out(pool, c)

                    def negative(c):
                        if c >= 2:
                            pool.wait_ge(h_out, c + 1)
                            pool.wait_ge(enc_s, c)
                            pool.tensor_scalar(e_sb[:], h_sb[:, c % 2], 0.0, None, ALU.min).then_inc(min_s, 1)

                    def residual(c):
                        if c == 0:
                            pool.wait_ge(b_in, 64)
                        pool.wait_ge(xb_in[c], 16)
                        pool.tensor_tensor(spare(c), spare(c), b4_sb[:].unsqueeze(1).broadcast_to([P, TC, F]), ALU.add).then_inc(xb_s, 1)

                    def deviation(c):
                        pool.wait_ge(mean_s, TC * (c + 1))
                        pool.tensor_tensor(rstd[:], mv[:, :, 1], eps[:], ALU.add).then_inc(var_s, 1)
                        pool.wait_ge(var_s, c + 1)
                        pool.tensor_tensor(rstd[:], rstd[:], half[:], ALU.pow).then_inc(rstd_s, 1)

                    steps([(-1, heads), (0, residual), (-1, negative), (1, deviation)])

                @block.vector
                def _(dve):
                    def inverse(c):
                        if c:
                            dve.wait_ge(h_out, c)
                        dve.reciprocal(rden[:], num[:, c * TC:(c + 1) * TC, :, D]).then_inc(rden_s, 1)
                        if c == 0:
                            heads_out(dve, c)

                    def negative(c):
                        if c < 2:
                            dve.wait_ge(h_out, c + 1)
                            if c:
                                dve.wait_ge(enc_s, c)
                            dve.tensor_scalar(e_sb[:], h_sb[:, c % 2], 0.0, None, ALU.min).then_inc(min_s, 1)
                        if c == 0:
                            dve.wait_ge(min_s, 1)
                            dve.tensor_scalar(h_sb[:, c % 2], h_sb[:, c % 2], 0.0, None, ALU.max).then_inc(exp_s, 1)

                    def cut_weights(c):
                        if c == 0:
                            for i, (name, src, k, m_) in enumerate(layers):
                                dve.wait_ge(raw_hi, i + 1)
                                dve.tensor_tensor(cut[name][1][:], raw[name], cut[name][0][:].bitcast(F32), ALU.subtract).then_inc(raw_lo, 1)

                    def elu(c):
                        dve.wait_ge(exp_s, 2 * c + 2)
                        dve.scalar_tensor_tensor(h_sb[:, c % 2], e_sb[:], -1.0, h_sb[:, c % 2], ALU.add, ALU.add).then_inc(enc_s, 1)

                    def enc_lo(c):
                        for f in range(KF):
                            dve.wait_ge(e_hi, c * KF + f + 1)
                            dve.tensor_tensor(et_lo[:, f, :], p_t[:, f, :], et_hi[:, f, :].bitcast(F32), ALU.subtract).then_inc(e_lo, 1)

                    def hidden_lo(c, first, slots):
                        for n, slot in enumerate(slots, first):
                            dve.wait_ge(y_act, c * 10 + 2 * n + 2)
                            dve.tensor_tensor(y_lo[:, slot, :], y_f[:, slot, :], y_hi[:, slot, :].bitcast(F32), ALU.subtract).then_inc(y_cut, 1)

                    def layer_out(c):
                        dve.wait_ge(xb_s, c + 1)
                        for i in range(TC):
                            dve.wait_ge(mm_done, c * 9 + 6 + i)
                            dve.tensor_tensor(x2[:, c * TC + i, :], p_m[:, i, :], spare(c)[:, i, :], ALU.add).then_inc(x2_s, 1)
                            dve.wait_ge(x2_s, c * TC + i + 1)
                            dve.bn_stats(stats[:, i, :], x2[:, c * TC + i, :]).then_inc(stat_s, 1)
                        for i in range(TC):
                            dve.wait_ge(stat_s, c * TC + i + 1)
                            dve.bn_aggr(mv[:, i, :], stats[:, i, :]).then_inc(mean_s, 1)

                    def norm(c):
                        dve.wait_ge(rstd_s, c + 1)
                        for i in range(TC):
                            dve.tensor_scalar(spare(c)[:, i, :], x2[:, c * TC + i, :], mv[:, i, 0:1], rstd[:, i:i + 1],
                                              ALU.subtract, ALU.mult).then_inc(xn2_s, 1)

                    def norm_lo(c):
                        for f in range(KF):
                            dve.wait_ge(n_hi, c * KF + f + 1)
                            dve.tensor_tensor(et_lo[:, f, :], p_t[:, f, :], et_hi[:, f, :].bitcast(F32), ALU.subtract).then_inc(n_lo, 1)

                    chosen = [0]

                    def early_choice(c):
                        if c == 0 or c == NC - 1:
                            return
                        if chosen[0] == 0:
                            dve.wait_ge(small_in, 48)
                            dve.wait_ge(enc_s, NC)
                        tiles = slice(0 if c == 1 else c * TC, (c + 1) * TC)
                        size = (tiles.stop - tiles.start) * E * E
                        flat = e_sb[:].rearrange("p t f -> p (t f)")
                        dve.wait_ge(g_out, c + 1)
                        for ins in choose(dve, tiles, flat[:, 0:size], flat[:, size:2 * size]):
                            ins.then_inc(choice_s, 1)
                            chosen[0] += 1
                            dve.wait_ge(choice_s, chosen[0])

                    steps([(2, norm), (3, early_choice), (-1, inverse), (1, lambda c: hidden_lo(c, 0, (0, 1))), (2, norm_lo),
                           (1, lambda c: hidden_lo(c, 2, (0,))), (0, elu), (0, cut_weights), (1, lambda c: hidden_lo(c, 3, (1, 0))),
                           (0, enc_lo), (-1, negative), (1, layer_out)])

                @block.scalar
                def _(act):
                    def cut_weights(c):
                        if c == 0:
                            for i, (name, src, k, m_) in enumerate(layers):
                                act.wait_ge(raw_in[i], 16)
                                act.activation(cut[name][0][:], raw[name], ACT.Copy).then_inc(raw_hi, 1)
                            act.wait_ge(b_in, 64)

                    def exp(c):
                        act.wait_ge(min_s, c + 1)
                        act.activation(e_sb[:], e_sb[:], ACT.Exp).then_inc(exp_s, 1)
                        if c:
                            act.activation(h_sb[:, c % 2], h_sb[:, c % 2], ACT.Relu).then_inc(exp_s, 1)

                    def enc_hi(c):
                        for f in range(KF):
                            act.wait_ge(turned, c * KF + f + 1)
                            act.activation(et_hi[:, f, :], p_t[:, f, :], ACT.Copy).then_inc(e_hi, 1)

                    hidden = [(0, b1_sb[:, 0:1], 0), (1, b1_sb[:, 1:2], 1), (2, b2_sb[:, 0:1], 0),
                              (0, b3_sb[:, 0:1], 1), (1, b3_sb[:, 1:2], 0)]

                    def relu(c, which):
                        for n in which:
                            bank, bias, slot = hidden[n]
                            act.wait_ge(mm_done, c * 9 + n + 1)
                            act.activation(y_f[:, slot, :], p_m[:, bank, :], ACT.Relu, bias=bias).then_inc(y_act, 1)
                            act.activation(y_hi[:, slot, :], p_m[:, bank, :], ACT.Relu, bias=bias).then_inc(y_act, 1)

                    def norm_hi(c):
                        for f in range(KF):
                            act.wait_ge(turned2, c * KF + f + 1)
                            act.activation(et_hi[:, f, :], p_t[:, f, :], ACT.Copy).then_inc(n_hi, 1)

                    def rows_out(c):
                        act.wait_ge(g_done, c + 1)
                        act.wait_ge(y_cut, (c + 1) * 5 + 3 if c + 1 < NC else NC * 5)
                        act.activation(g_rows, p_m[0:E, 3, :], ACT.Copy).then_inc(gr_out, 1)

                    def scores_out(c):
                        act.wait_ge(g_turned, c + 1)
                        act.activation(scores[:, c * TC:(c + 1) * TC, :], p_m[:, 3, 0:TC * E].rearrange("p (t e) -> p t e", e=E),
                                       ACT.Copy).then_inc(g_out, 1)

                    steps([(0, cut_weights), (1, lambda c: relu(c, (0, 1))), (2, norm_hi), (1, lambda c: relu(c, (2,))),
                           (2, rows_out), (1, lambda c: relu(c, (3,))), (2, scores_out), (1, lambda c: relu(c, (4,))), (0, enc_hi), (-1, exp)])

                @block.tensor
                def _(pe):
                    def product(dst, name, o, k, hi, lo):
                        w_h, w_l = cut[name]
                        for n, (l, r) in enumerate([(w_h, hi), (w_l, hi), (w_h, lo)]):
                            for f in range(k):
                                mm = pe.matmul(dst, l[:, f, o * P:(o + 1) * P], r[:, f, :], start=(n + f == 0), stop=(n == 2 and f == k - 1))
                        return mm

                    def turn(src, done):
                        for f in range(KF):
                            for i in range(TC):
                                mm = pe.transpose(p_t[:, f, i * P:(i + 1) * P], src[:, i, f * P:(f + 1) * P], id_sb[:])
                            mm.then_inc(done, 1)

                    def turn_enc(c):
                        pe.wait_ge(enc_s, c + 1)
                        if c >= 2:
                            pe.wait_ge(n_lo, (c - 1) * KF)
                        turn(h_sb[:, c % 2], turned)

                    def layer1(c):
                        if c == 0:
                            pe.wait_ge(raw_lo, len(layers))
                        pe.wait_ge(e_lo, (c + 1) * KF)
                        if c:
                            pe.wait_ge(x2_s, c * TC - 2)
                        for o in range(F1 // P):
                            product(p_m[:, o, :], "w1", o, KF, et_hi, et_lo).then_inc(mm_done, 1)

                    def layer2(c):
                        pe.wait_ge(y_cut, c * 5 + 2)
                        if c:
                            pe.wait_ge(x2_s, c * TC)
                        product(p_m[:, 2, :], "w2", 0, 2, y_hi, y_lo).then_inc(mm_done, 1)

                    def layer3(c):
                        pe.wait_ge(y_cut, c * 5 + 3)
                        for o in range(F3 // P):
                            product(p_m[:, o, :], "w3", o, 1, y_hi, y_lo).then_inc(mm_done, 1)

                    def layer4(c):
                        pe.wait_ge(y_cut, c * 5 + 5)
                        if c:
                            pe.wait_ge(g_out, c)
                        w_h, w_l = cut["w4"]
                        for i in range(TC):
                            for n, (l, r) in enumerate([(y_hi, w_h), (y_hi, w_l), (y_lo, w_h)]):
                                for f in range(2):
                                    mm = pe.matmul(p_m[:, i, :], l[:, 1 - f, i * P:(i + 1) * P], r[:, f, :],
                                                   start=(n + f == 0), stop=(n == 2 and f == 1))
                            mm.then_inc(mm_done, 1)

                    def turn_norm(c):
                        pe.wait_ge(xn2_s, (c + 1) * TC)
                        if c + 1 < NC:
                            pe.wait_ge(e_lo, (c + 2) * KF)
                        turn(spare(c), turned2)

                    def gate(c):
                        pe.wait_ge(n_lo, (c + 1) * KF)
                        w_h, w_l = cut["gate"]
                        for n, (l, r) in enumerate([(w_h, et_hi), (w_l, et_hi), (w_h, et_lo)]):
                            for f in range(KF):
                                mm = pe.matmul(p_m[0:E, 3, :], l[:, f, :], r[:, f, :], start=(n + f == 0), stop=(n == 2 and f == KF - 1))
                        mm.then_inc(g_done, 1)

                    def turn_scores(c):
                        pe.wait_ge(gr_out, c + 1)
                        for i in range(TC):
                            mm = pe.transpose(p_m[:, 3, i * E:(i + 1) * E], g_rows[:, i * P:(i + 1) * P], id_sb[0:E, 0:E])
                        mm.then_inc(g_turned, 1)

                    steps([(1, layer1), (2, turn_norm), (1, layer2), (2, gate), (1, layer3), (2, turn_scores), (0, turn_enc), (1, layer4)])

        sums_kept.close()
        raw_kept.close()

        with ExitStack() as st:
            ew_lo = sb(st, "ew_lo", [P, E, KF, F], F32R)
            ew_hi = sb(st, "ew_hi", [P, E, KF, F], F32R)
            xt_hi = sb(st, "xt_hi2", [P, XR, F], F32R)
            xt_lo = sb(st, "xt_lo2", [P, XR, F], F32R)
            ring = sb(st, "ring", [P, 2 * XR, F])
            eb_bc = sb(st, "eb_bc", [P, E, F])
            route_sb = sb(st, "route_sb", [P, P + NS + 1 + NT + 1])
            iota_bf = sb(st, "iota_bf", [P, P], BF16)
            tile_t_bf = sb(st, "tile_t_bf", [P, NT], BF16)
            rest_bf = sb(st, "rest_bf", [P, 2 * NT], BF16)
            sel_bf = sb(st, "sel_bf", [P, NT + 1, E], BF16)
            pr = sb(st, "pr", [P, NT, E])
            col = sb(st, "col", [P, 4, NT])
            ahead = sb(st, "ahead", [P, NT + 1, E])
            pos_e = sb(st, "pos_e", [P, NT, E])
            base = sb(st, "base", [P, 2, E])
            pos = sb(st, "pos", [P, 2, NT])
            tile_no = sb(st, "tile_no", [P, 2 * NT])
            wts = sb(st, "wts", [P, 2, NT])
            pos_u = sb(st, "pos_u", [P, 2, NT], mybir.dt.uint32)
            ids = sb(st, "ids", [P, NS], mybir.dt.uint32)
            used = sb(st, "used", [P, 1])
            stores = sb(st, "stores", [P, XR], mybir.dt.int32)
            slot_e = sb(st, "slot_e", [P, NS], mybir.dt.int32)
            p_t = ps(st, "p_t2", [P, XR, F])
            p_y = ps(st, "p_y", [P, XR, F])
            p_r = ps(st, "p_r", [P, F])

            xg, y_ring = ring[:, 0:XR, :], ring[:, XR:2 * XR, :]
            work = ring[:].rearrange("p r f -> p (r f)")
            gt, eq = work[:, 0:TC * E * E], work[:, TC * E * E:2 * TC * E * E]
            ge = work[:, 0:NT * (NS + 1)].bitcast(BF16).rearrange("p (t s) -> p t s", t=2 * NT)
            cmp = work[:, 2 * NT * (NS + 1):][:, 0:NS * E]
            cmp_n = cmp[:, 0:E * NT].rearrange("p (e k) -> p e k", e=E)
            cmp_e = cmp[:, 0:E * E].rearrange("p (e f) -> p e f", e=E)
            cmp_s = cmp.rearrange("p (s e) -> p s e", e=E)
            QW = 2 * NT * NS
            one_q = work[:, 2 * XR * F - QW:].bitcast(BF16).rearrange("p (t a s) -> p t a s", t=2 * NT, a=2)
            one_r = eb_bc[:, E // 2:, :].rearrange("p e f -> p (e f)").bitcast(BF16).rearrange("p (t r) -> p t r", t=2 * NT)
            own_q = eb_bc[:, 0:E // 2, :].rearrange("p e f -> p (e f)")[:, 0:QW // 2].bitcast(BF16).rearrange("p (t s) -> p t s", t=2 * NT)

            def back(i):
                r = i % GB
                return xg[:, r, :] if r < XR else eb_bc[:, r - XR, :]

            iota_r = route_sb[:, 0:P]
            bound = route_sb[:, P:P + NS + 1]
            tile_t = route_sb[:, P + NS + 1:P + NS + 1 + NT]
            own_p = route_sb[:, P + NS + 1 + NT:P + NS + 2 + NT]

            eb_in, sc_step, ex2_s, ewhi_s, ewlo_s = sem("eb_in"), sem("sc_step"), sem("ex2_s"), sem("ewhi_s"), sem("ewlo_s")
            prefix_done, node_done, q_scaled, ids_done = sem("prefix_done"), sem("node_done"), sem("q_scaled"), sem("ids_done")
            xg_in = [sem(f"xg_in{r}") for r in range(XR)]
            turned3, xthi_s, xtlo_s, y_done, y_s = sem("turned3"), sem("xthi_s"), sem("xtlo_s"), sem("y_done"), sem("y_s")
            y_out = [sem(f"y_out{r}") for r in range(XR)]
            GB = XR + E
            route_in, carried = sem("route_in"), sem("carried")
            back_in = [sem(f"back_in{i}") for i in range(GB)]
            mixed, out_s = sem("mixed"), sem("out_s")
            AT_SEL, AT_PR, AT_Q, AT_R, AT_STORES = 9, 11, 27, 31, 53
            DVE_CUTS = (1, 4, 6, 7)

            def slot_tiles(eng, body):
                with eng.Fori(0, NS // XR - 1) as k:
                    for r in range(XR):
                        body(k * XR + r, k, r, False)
                for r in range(XR):
                    body(NS - XR + r, NS // XR - 1, r, r == XR - 1)

            with nc.Block() as block:
                @block.sync
                def _(sp):
                    sp.wait_ge(xn2_out, 16 * NC)
                    sp.dma_start(route_sb[:], route).then_inc(route_in, 16)
                    sp.wait_ge(node_done, 1)
                    for e in range(E):
                        sp.dma_start(eb_bc[:, e, :], expert_b[e].partition_broadcast(P)).then_inc(eb_in, 16)

                    def body(s, k, r, last):
                        sp.wait_ge(y_s, s + 1 + XR)
                        sp.dma_start(y_d.rearrange("(s p) f -> s p f", p=P)[bass.ds(s, 1)].rearrange("a p f -> p (a f)"),
                                     y_ring[:, r, :]).then_inc(y_out[r], 16)

                    slot_tiles(sp, body)
                    for t in range(NT):
                        sp.wait_ge(mixed, 2 * t + 2)
                        sp.dma_start(out_tiles[:, t, :], x2[:, t, :]).then_inc(out_s, 16)
                    sp.wait_ge(out_s, 16 * NT)

                @block.gpsimd
                def _(pool):
                    for e in range(E):
                        if e not in DVE_CUTS:
                            pool.wait_ge(ewhi_s, e + 1)
                            pool.tensor_tensor(ew_lo[:, e], ew_raw[:, e], ew_hi[:, e].bitcast(F32), ALU.subtract).then_inc(ewlo_s, 1)
                    pool.wait_ge(xn2_out, 16 * NC)
                    pool.wait_ge(ids_done, 1)
                    for s in range(NS):
                        if s >= XR:
                            pool.wait_ge(turned3, s - XR + 1)
                        pool.indirect_dma_start(xg[:, s % XR, :], None, xn2_d,
                                                bass.IndirectOffsetOnAxis(ap=ids[:, s:s + 1], axis=0)).then_inc(xg_in[s % XR], 16)
                    pool.wait_ge(sc_step, AT_STORES)
                    full = [pool.value_load(stores[0:1, r:r + 1], min_val=16 * (TOPK * NT // XR + 1), max_val=16 * (NS // XR + 1))
                            for r in range(XR)]
                    for r in range(XR):
                        pool.wait_ge(y_out[r], full[r])
                        pool.sem_inc(carried, 1)
                    pool.wait_ge(turned3, NS)
                    for i in range(2 * NT):
                        if i == XR:
                            pool.wait_ge(y_s, NS + XR)
                        if i >= GB:
                            pool.wait_ge(mixed, i - GB + 1)
                        pool.indirect_dma_start(back(i), None, y_d,
                                                bass.IndirectOffsetOnAxis(ap=pos_u[:, i % 2, i // 2:i // 2 + 1], axis=0)).then_inc(back_in[i % GB], 16)

                @block.scalar
                def _(act):
                    act.wait_ge(ew_in, 16 * E)

                    def cut_hi(e):
                        act.activation(ew_hi[:, e], ew_raw[:, e], ACT.Copy).then_inc(ewhi_s, 1)

                    for e in range(3):
                        cut_hi(e)
                    act.wait_ge(sc_step, AT_PR)
                    act.activation(pr[:], pr[:], ACT.Exp).then_inc(ex2_s, 1)
                    for e in range(3, E):
                        cut_hi(e)
                    act.wait_ge(route_in, 16)
                    act.wait_ge(sc_step, AT_Q)
                    act.activation(one_q[:, :, 0, :], own_q, ACT.Copy, scale=own_p).then_inc(q_scaled, 1)

                    def body(s, k, r, last):
                        act.wait_ge(turned3, s + 1)
                        act.activation(xt_hi[:, r, :], p_t[:, r, :], ACT.Copy).then_inc(xthi_s, 1)

                    slot_tiles(act, body)

                @block.vector
                def _(dve):
                    steps = [0]

                    def step(ins):
                        steps[0] += 1
                        ins.then_inc(sc_step, 1)
                        dve.wait_ge(sc_step, steps[0])

                    def cut_lo(e):
                        dve.wait_ge(ewhi_s, e + 1)
                        dve.tensor_tensor(ew_lo[:, e], ew_raw[:, e], ew_hi[:, e].bitcast(F32), ALU.subtract).then_inc(ewlo_s, 1)

                    for r in range(XR):
                        dve.sem_inc(y_out[r], 16)
                    dve.sem_inc(y_s, XR)
                    last = slice(NT - TC, NT)
                    dve.wait_ge(xn2_out, 16 * NC)
                    for ins in choose(dve, last, gt, eq):
                        step(ins)
                    dve.memset(sel_bf[:, NT, :], 0.0)
                    dve.wait_ge(route_in, 16)
                    dve.tensor_copy(iota_bf[:], iota_r)
                    dve.tensor_copy(tile_t_bf[:], tile_t)
                    step(dve.tensor_copy(sel_bf[:, 0:NT, :], sel[:]))
                    assert steps[0] == AT_SEL
                    step(dve.tensor_reduce(col[:, 0, :], scores[:], AX.X, ALU.max))
                    step(dve.tensor_tensor(pr[:], scores[:], col[:, 0, :].unsqueeze(2).broadcast_to([P, NT, E]), ALU.subtract))
                    assert steps[0] == AT_PR
                    cut_lo(DVE_CUTS[0])
                    dve.wait_ge(prefix_done, 1)
                    step(dve.tensor_copy(ahead[:], p_r[:, 0:(NT + 1) * E].rearrange("p (t e) -> p t e", e=E)))
                    step(dve.tensor_tensor(cmp_n, ahead[:, NT, :].unsqueeze(2).broadcast_to([P, E, NT]),
                                           bound[:, 0:NT].unsqueeze(1).broadcast_to([P, E, NT]), ALU.is_gt))
                    step(dve.tensor_reduce(base[:, 0, :], cmp_n, AX.X, ALU.add))
                    step(dve.tensor_reduce(used[:], base[:, 0, :], AX.X, ALU.add))
                    tri_e = tri[:].rearrange("p (e f) -> p e f", e=E)
                    step(dve.tensor_tensor(cmp_e, tri_e, base[:, 0:1, :].broadcast_to([P, E, E]), ALU.mult))
                    step(dve.tensor_reduce(base[:, 0, :], cmp_e, AX.X, ALU.add))
                    step(dve.tensor_scalar(base[:, 1, :], base[:, 0, :], float(P), None, ALU.mult))
                    step(dve.tensor_tensor(pos_e[:], ahead[:, 0:NT, :], base[:, 1:2, :].broadcast_to([P, NT, E]), ALU.add))
                    step(dve.tensor_tensor(pos_e[:], pos_e[:], sel[:], ALU.mult))
                    step(dve.tensor_reduce(pos[:, 1, :], pos_e[:], AX.X, ALU.max))
                    step(dve.tensor_reduce(pos[:, 0, :], pos_e[:], AX.X, ALU.add))
                    step(dve.tensor_tensor(pos[:, 0, :], pos[:, 0, :], pos[:, 1, :], ALU.subtract))
                    by_node = pos[:].rearrange("p a t -> p (a t)")
                    step(dve.tensor_tensor(ge, by_node.unsqueeze(2).broadcast_to([P, 2 * NT, NS + 1]),
                                           bound.unsqueeze(1).broadcast_to([P, 2 * NT, NS + 1]), ALU.is_ge))
                    step(dve.tensor_reduce(tile_no[:], ge, AX.X, ALU.add))
                    step(dve.scalar_tensor_tensor(rest_bf[:], tile_no[:], -float(P), by_node, ALU.mult, ALU.add))
                    step(dve.tensor_tensor(own_q, ge[:, :, 0:NS], ge[:, :, 1:NS + 1], ALU.subtract))
                    assert steps[0] == AT_Q
                    for a in range(2):
                        at = slice(a * NT, (a + 1) * NT)
                        step(dve.tensor_tensor(one_q[:, at, 1, :], own_q[:, at, :], tile_t_bf[:].unsqueeze(2).broadcast_to([P, NT, NS]), ALU.mult))
                    for a in range(2):
                        at = slice(a * NT, (a + 1) * NT)
                        step(dve.tensor_tensor(one_r[:, at, :], iota_bf[:].unsqueeze(1).broadcast_to([P, NT, P]),
                                               rest_bf[:, at].unsqueeze(2).broadcast_to([P, NT, P]), ALU.is_equal))
                    assert steps[0] == AT_R
                    step(dve.tensor_tensor(cmp_s, base[:, 1:2, :].broadcast_to([P, NS, E]), bound[:, 0:NS].unsqueeze(2).broadcast_to([P, NS, E]), ALU.is_le))
                    begun = col[:].rearrange("p a t -> p (a t)")[:, 0:NS]
                    step(dve.tensor_reduce(begun, cmp_s, AX.X, ALU.add))
                    step(dve.tensor_scalar(slot_e[:], begun, -1.0, None, ALU.add))
                    dve.wait_ge(node_done, 1)
                    step(dve.tensor_copy(ahead[:].rearrange("p t e -> p (t e)")[:, 0:2 * NS], p_r[:, 256:256 + 2 * NS]))
                    by_slot = ahead[:].rearrange("p t e -> p (t e)")[:, 0:2 * NS].rearrange("p (a s) -> p a s", a=2)
                    dve.scalar_tensor_tensor(ids[:], by_slot[:, 1, :], float(P), by_slot[:, 0, :], ALU.mult, ALU.add).then_inc(ids_done, 1)
                    for e in DVE_CUTS[1:]:
                        cut_lo(e)

                    def lo(s, r):
                        dve.wait_ge(xthi_s, s + 1)
                        dve.tensor_tensor(xt_lo[:, r, :], p_t[:, r, :], xt_hi[:, r, :].bitcast(F32), ALU.subtract).then_inc(xtlo_s, 1)

                    def body(s, k, r, last):
                        if not last:
                            lo(s + 1, (r + 1) % XR)
                        dve.wait_ge(y_done, s + 1)
                        dve.wait_ge(y_out[r], k * 16 + 16)
                        e = dve.value_load(slot_e[0:1, bass.ds(s, 1)], min_val=0, max_val=E - 1)
                        dve.tensor_tensor(y_ring[:, r, :], p_y[:, r, :], eb_bc[:, bass.ds(e, 1), :].rearrange("p a f -> p (a f)"),
                                          ALU.add).then_inc(y_s, 1)

                    lo(0, 0)
                    dve.wait_ge(ex2_s, 1)
                    step(dve.tensor_reduce(col[:, 1, :], pr[:], AX.X, ALU.add))
                    step(dve.reciprocal(col[:, 1, :], col[:, 1, :]))
                    step(dve.tensor_tensor(pr[:], pr[:], col[:, 1, :].unsqueeze(2).broadcast_to([P, NT, E]), ALU.mult))
                    step(dve.scalar_tensor_tensor(pr[:], pr[:], W_THRES, sel[:], ALU.max, ALU.mult))
                    step(dve.tensor_reduce(col[:, 2, :], pr[:], AX.X, ALU.add))
                    step(dve.tensor_scalar(col[:, 2, :], col[:, 2, :], float(TOPK), None, ALU.mult))
                    step(dve.reciprocal(col[:, 3, :], col[:, 2, :]))
                    step(dve.tensor_tensor(pr[:], pr[:], col[:, 3, :].unsqueeze(2).broadcast_to([P, NT, E]), ALU.mult))
                    step(dve.tensor_tensor(pos_e[:], pos_e[:], pos[:, 1, :].unsqueeze(2).broadcast_to([P, NT, E]), ALU.is_equal))
                    step(dve.tensor_tensor(pos_e[:], pr[:], pos_e[:], ALU.mult))
                    step(dve.tensor_tensor(pr[:], pr[:], pos_e[:], ALU.subtract))
                    step(dve.tensor_reduce(wts[:, 1, :], pos_e[:], AX.X, ALU.add))
                    step(dve.tensor_reduce(wts[:, 0, :], pr[:], AX.X, ALU.add))
                    step(dve.tensor_copy(pos_u[:], pos[:]))
                    step(dve.tensor_scalar(used[:], used[:], float(P), None, ALU.mult))
                    in_use = pos_e[:].rearrange("p t e -> p (t e)")[:, 0:NS]
                    step(dve.tensor_tensor(in_use, bound[:, 0:NS], used[:].broadcast_to([P, NS]), ALU.is_lt))
                    step(dve.tensor_reduce(tile_no[:, 0:XR], in_use.rearrange("p (k r) -> p r k", r=XR), AX.X, ALU.add))
                    step(dve.tensor_scalar(stores[:], tile_no[:, 0:XR], 16.0, 16.0, ALU.mult, ALU.add))
                    assert steps[0] == AT_STORES
                    dve.wait_ge(eb_in, 16 * E)
                    slot_tiles(dve, body)
                    for t in range(NT):
                        for a in range(2):
                            i = 2 * t + a
                            dve.wait_ge(back_in[i % GB], 16 * (i // GB + 1))
                            if a:
                                dve.wait_ge(mixed, i)
                            dve.scalar_tensor_tensor(x2[:, t, :], back(i), wts[:, a, t:t + 1], x2[:, t, :],
                                                     ALU.mult, ALU.add).then_inc(mixed, 1)

                @block.tensor
                def _(pe):
                    pe.wait_ge(small_in, 48)
                    pe.wait_ge(sc_step, AT_SEL)
                    counts = p_r[:, 0:(NT + 1) * E].rearrange("p (t e) -> p t e", e=E)
                    pe.matmul(counts, prefix_sb[:, 0, :], sel_bf[:], start=True, stop=False, skip_group_check=True)
                    for t in range(NT):
                        mm = pe.matmul(counts[:, t + 1:, :], prefix_sb[:, 1, :], sel_bf[:, t:t + 1, :].broadcast_to([P, NT - t, E]),
                                       start=False, stop=(t == NT - 1), skip_group_check=True)
                    mm.then_inc(prefix_done, 1)
                    pe.wait_ge(q_scaled, 1)
                    for i in range(2 * NT):
                        if i % NT == 0:
                            pe.wait_ge(sc_step, AT_R - 1 + i // NT)
                        mm = pe.matmul(p_r[:, 256:256 + 2 * NS], one_r[:, i, :], one_q[:, i].rearrange("p a s -> p (a s)"),
                                       start=(i == 0), stop=(i == 2 * NT - 1))
                    mm.then_inc(node_done, 1)

                    def turn(k, r):
                        pe.wait_ge(xg_in[r], k * 16 + 16)
                        for f in range(KF):
                            mm = pe.transpose(p_t[:, r, f * P:(f + 1) * P], xg[:, r, f * P:(f + 1) * P], id_sb[:])
                        mm.then_inc(turned3, 1)

                    def body(s, k, r, last):
                        if not last:
                            turn(k + (r + 1) // XR, (r + 1) % XR)
                        e = pe.value_load(slot_e[0:1, bass.ds(s, 1)], min_val=0, max_val=E - 1)
                        pe.wait_ge(xtlo_s, s + 1)
                        pe.wait_ge(y_s, s + 1)
                        for f in range(KF):
                            hi, lo = xt_hi[:, r, f * P:(f + 1) * P], xt_lo[:, r, f * P:(f + 1) * P]
                            w_h, w_l = (w_[:, bass.ds(e, 1), f, :].rearrange("p a f -> p (a f)") for w_ in (ew_hi, ew_lo))
                            pe.matmul(p_y[:, r, :], hi, w_h, start=(f == 0), stop=False)
                            pe.matmul(p_y[:, r, :], hi, w_l, start=False, stop=False)
                            mm = pe.matmul(p_y[:, r, :], lo, w_h, start=False, stop=(f == KF - 1))
                        mm.then_inc(y_done, 1)

                    turn(0, 0)
                    pe.wait_ge(ewlo_s, E)
                    slot_tiles(pe, body)
        late.close()
    return nc


def kernel(x, adj, L0_gnn_W, L0_gnn_a1, L0_gnn_a2, L0_gnn_W1, L0_gnn_b1, L0_gnn_W2, L0_gnn_b2, L0_gnn_W3, L0_gnn_b3,
           L0_gnn_W4, L0_gnn_b4, L0_ffn_gate_W, L0_ffn_gate_b, L0_ffn_expert_W, L0_ffn_expert_b):
    import ml_dtypes
    import numpy as np
    from concourse import bacc
    from concourse.bass_utils import run_bass_kernel_spmd

    head_pick = np.zeros((96, H + 1, P), np.float32)
    for k in range(3):
        for h in range(H + 1):
            head_pick[32 * k + h, h] = 1.0
    by_p = lambda row: np.broadcast_to(row.astype(np.float32), (P, row.size))
    route = np.concatenate([by_p(np.arange(P) - P), by_p(P * np.arange(NS + 1)), by_p(np.arange(NT)),
                            np.arange(P, dtype=np.float32)[:, None]], axis=1)
    prefix = np.concatenate([np.triu(np.ones((P, P)), 1), np.ones((P, P))], axis=1).astype(ml_dtypes.bfloat16)
    arrays = {
        "x": np.asarray(x),
        "adj_t": np.asarray(adj).T,
        "w": np.asarray(L0_gnn_W).transpose(1, 0, 2).reshape(F, H * D),
        "a1": np.asarray(L0_gnn_a1).reshape(-1), "a2": np.asarray(L0_gnn_a2).reshape(-1),
        "w1": np.asarray(L0_gnn_W1).T, "b1": np.asarray(L0_gnn_b1).reshape(-1, P).T,
        "w2": np.asarray(L0_gnn_W2).T, "b2": np.asarray(L0_gnn_b2).reshape(-1, P).T,
        "w3": np.asarray(L0_gnn_W3).T, "b3": np.asarray(L0_gnn_b3).reshape(-1, P).T,
        "w4": np.asarray(L0_gnn_W4).T, "b4": np.asarray(L0_gnn_b4),
        "gate_w": np.asarray(L0_ffn_gate_W), "gate_b": np.asarray(L0_ffn_gate_b),
        "expert_w": np.asarray(L0_ffn_expert_W), "expert_b": np.asarray(L0_ffn_expert_b),
        "ident": np.eye(P, dtype=np.float32),
        "head_pick": head_pick.reshape(96, (H + 1) * P).astype(ml_dtypes.bfloat16),
        "before": np.tril(np.ones((E, E), np.float32), -1).reshape(-1),
        "route": route, "prefix": prefix,
    }
    nc = bacc.Bacc("TRN2", target_bir_lowering=False, num_devices=1)
    feeds, aps = {}, []
    for name, a in arrays.items():
        a = np.ascontiguousarray(a)
        feeds["in_" + name] = a
        aps.append(nc.dram_tensor("in_" + name, a.shape, mybir.dt.from_np(a.dtype), kind="ExternalInput").ap())
    aps.append(nc.dram_tensor("out_x", (N, F), F32, kind="ExternalOutput").ap())
    layer_kernel(nc, *aps)
    r = run_bass_kernel_spmd(nc, [feeds], core_ids=[0])
    return r.results[0]["out_x"]
```
